# Optimizing a Trainium2 kernel written in Bass

```python
import numpy as np
import jax
import jax.numpy as jnp

def _softmax(x, axis=-1):
    return jax.nn.softmax(x, axis=axis)

def _gelu(x):
    return jax.nn.gelu(x, approximate=True)

def _silu(x):
    return jax.nn.silu(x)

def _sigmoid(x):
    return jax.nn.sigmoid(x)

def _layernorm(x, axis=-1, eps=1e-05):
    m = jnp.mean(x, axis=axis, keepdims=True)
    v = jnp.var(x, axis=axis, keepdims=True)
    return (x - m) / jnp.sqrt(v + eps)

def _scatter_add(tgt, idx, src, axis=0):
    return tgt.at[idx].add(src)

def _segment_sum(src, seg, n):
    return jax.ops.segment_sum(src, seg, n)
kernel_name = 'mk_vit_tower_d1_tok_img768_r4_bc7ff5'

def setup_inputs(seed: int=0):
    np.random.seed(seed)
    _w = jnp.asarray

    def _rec_inputs():
        import jax
        import jax.numpy as jnp
        _rk = jax.random.key(seed)
        x = -0.00016672 + 0.999947 * jax.random.normal(jax.random.fold_in(_rk, 1), (32, 3, 96, 96), jnp.float32)
        return x
    x = _rec_inputs()

    def _L0_tok_setup():
        import jax, jax.numpy as jnp
        import numpy as np
        P = 16
        EMBED = 192
        EPS = 1e-05

        def _patchify(x):
            N, C, H, W = x.shape
            x = x.reshape(N, C, H // P, P, W // P, P)
            x = x.transpose(0, 2, 4, 1, 3, 5)
            return x.reshape(N, H // P * (W // P), C * P * P)
        key = jax.random.key(seed)
        k1, k2, k3 = jax.random.split(key, 3)
        in_dim = P * P * 3
        x = jax.random.normal(k1, (64, 3, 96, 96), dtype=jnp.float32)
        bound = 1.0 / np.sqrt(in_dim)
        W = jax.random.uniform(k2, (EMBED, in_dim), dtype=jnp.float32, minval=-bound, maxval=bound)
        b = jax.random.uniform(k3, (EMBED,), dtype=jnp.float32, minval=-bound, maxval=bound)
        ln_w = jnp.ones((EMBED,), dtype=jnp.float32)
        ln_b = jnp.zeros((EMBED,), dtype=jnp.float32)
        return {'x': x, 'W': W, 'b': b, 'ln_w': ln_w, 'ln_b': ln_b}
    _L0_tok_all = _L0_tok_setup()
    _L0_tok_in = {k: v for k, v in _L0_tok_all.items() if k in ('W', 'b', 'ln_w', 'ln_b')}
    del _L0_tok_all

    def _L0_attn_setup():
        import jax, jax.numpy as jnp
        import numpy as np
        HEADS = 12
        DIM_HEAD = 64
        NUM_PATCHES = 64
        LN_EPS = 1e-05
        key = jax.random.key(seed)
        k0, k1, k2 = jax.random.split(key, 3)
        B, T, C = (2, 1024, 192)
        inner = HEADS * DIM_HEAD
        x = jax.random.normal(k0, (B, T, C), jnp.float32)
        ln_gamma = jnp.ones((C,), jnp.float32)
        ln_beta = jnp.zeros((C,), jnp.float32)
        w_qkv = jax.random.normal(k1, (3 * inner, C), jnp.float32) * 0.02
        w_out = jax.random.normal(k2, (C, inner), jnp.float32) * 0.02
        b_out = jnp.zeros((C,), jnp.float32)
        return {'x': x, 'ln_gamma': ln_gamma, 'ln_beta': ln_beta, 'w_qkv': w_qkv, 'w_out': w_out, 'b_out': b_out}
    _L0_attn_all = _L0_attn_setup()
    _L0_attn_in = {k: v for k, v in _L0_attn_all.items() if k in ('ln_gamma', 'ln_beta', 'w_qkv', 'w_out', 'b_out')}
    del _L0_attn_all

    def _L0_ffn_setup():
        import jax, jax.numpy as jnp
        import numpy as np
        B, L, D, E, F, K = (2, 256, 192, 16, 768, 2)
        key = jax.random.key(seed)
        ks = jax.random.split(key, 6)
        s = 0.02
        x = jax.random.normal(ks[0], (B, L, D), dtype=jnp.float32)
        wr = jax.random.normal(ks[1], (E, D), dtype=jnp.float32) * s
        w1 = jax.random.normal(ks[2], (E, F, D), dtype=jnp.float32) * s
        b1 = jnp.zeros((E, F), dtype=jnp.float32)
        w2 = jax.random.normal(ks[3], (E, D, F), dtype=jnp.float32) * s
        b2 = jnp.zeros((E, D), dtype=jnp.float32)
        return {'x': x, 'wr': wr, 'w1': w1, 'b1': b1, 'w2': w2, 'b2': b2}
    _L0_ffn_all = _L0_ffn_setup()
    _L0_ffn_in = {k: v for k, v in _L0_ffn_all.items() if k in ('wr', 'w1', 'b1', 'w2', 'b2')}
    del _L0_ffn_all
    return {'x': x, 'L0_tok_W': _L0_tok_in['W'], 'L0_tok_b': _L0_tok_in['b'], 'L0_tok_ln_w': _L0_tok_in['ln_w'], 'L0_tok_ln_b': _L0_tok_in['ln_b'], 'L0_attn_ln_gamma': _L0_attn_in['ln_gamma'], 'L0_attn_ln_beta': _L0_attn_in['ln_beta'], 'L0_attn_w_qkv': _L0_attn_in['w_qkv'], 'L0_attn_w_out': _L0_attn_in['w_out'], 'L0_attn_b_out': _L0_attn_in['b_out'], 'L0_ffn_wr': _L0_ffn_in['wr'], 'L0_ffn_w1': _L0_ffn_in['w1'], 'L0_ffn_b1': _L0_ffn_in['b1'], 'L0_ffn_w2': _L0_ffn_in['w2'], 'L0_ffn_b2': _L0_ffn_in['b2']}

def reference(x, L0_tok_W, L0_tok_b, L0_tok_ln_w, L0_tok_ln_b, L0_attn_ln_gamma, L0_attn_ln_beta, L0_attn_w_qkv, L0_attn_w_out, L0_attn_b_out, L0_ffn_wr, L0_ffn_w1, L0_ffn_b1, L0_ffn_w2, L0_ffn_b2):
    import jax
    import jax.numpy as jnp

    def _L0_tok_ref(x, W, b, ln_w, ln_b):
        import jax, jax.numpy as jnp
        import numpy as np
        P = 16
        EMBED = 192
        EPS = 1e-05

        def _patchify(x):
            N, C, H, W = x.shape
            x = x.reshape(N, C, H // P, P, W // P, P)
            x = x.transpose(0, 2, 4, 1, 3, 5)
            return x.reshape(N, H // P * (W // P), C * P * P)
        patches = _patchify(x)
        y = jnp.einsum('nsi,oi->nso', patches, W) + b
        mu = jnp.mean(y, axis=-1, keepdims=True)
        var = jnp.mean(jnp.square(y - mu), axis=-1, keepdims=True)
        return (y - mu) / jnp.sqrt(var + EPS) * ln_w + ln_b

    def _L0_attn_ref(x, ln_gamma, ln_beta, w_qkv, w_out, b_out):
        import jax, jax.numpy as jnp
        import numpy as np
        HEADS = 12
        DIM_HEAD = 64
        NUM_PATCHES = 64
        LN_EPS = 1e-05
        B, T, C = x.shape
        scale = DIM_HEAD ** (-0.5)
        mu = jnp.mean(x, axis=-1, keepdims=True)
        var = jnp.mean(jnp.square(x - mu), axis=-1, keepdims=True)
        xn = (x - mu) * jax.lax.rsqrt(var + LN_EPS) * ln_gamma + ln_beta
        qkv = jnp.einsum('btc,oc->bto', xn, w_qkv)
        q, k, v = jnp.split(qkv, 3, axis=-1)

        def to_heads(t):
            return t.reshape(B, T, HEADS, DIM_HEAD).transpose(0, 2, 1, 3)
        q, k, v = (to_heads(q), to_heads(k), to_heads(v))
        dots = jnp.einsum('bhtd,bhsd->bhts', q, k) * scale
        frame = jnp.arange(T) // NUM_PATCHES
        mask = frame[:, None] >= frame[None, :]
        dots = jnp.where(mask, dots, -jnp.inf)
        attn = jax.nn.softmax(dots, axis=-1)
        out = jnp.einsum('bhts,bhsd->bhtd', attn, v)
        out = out.transpose(0, 2, 1, 3).reshape(B, T, HEADS * DIM_HEAD)
        return jnp.einsum('bti,oi->bto', out, w_out) + b_out

    def _L0_ffn_ref(x, wr, w1, b1, w2, b2):
        import jax, jax.numpy as jnp
        import numpy as np
        B, L, D, E, F, K = (2, 256, 192, 16, 768, 2)
        logits = jnp.einsum('bld,ed->ble', x, wr)
        probs = jax.nn.softmax(logits, axis=-1)
        top_p, ix = jax.lax.top_k(probs, K)
        gate = jnp.sum(jax.nn.one_hot(ix, E, dtype=x.dtype) * top_p[..., None], axis=-2)
        h = jnp.einsum('bld,efd->blef', x, w1) + b1
        h = jax.nn.gelu(h, approximate=False)
        y = jnp.einsum('blef,edf->bled', h, w2) + b2
        out = x + jnp.einsum('bled,ble->bld', y, gate)
        return out
    h = _L0_tok_ref(x, L0_tok_W, L0_tok_b, L0_tok_ln_w, L0_tok_ln_b)
    h = h + _L0_attn_ref(_layernorm(h, axis=-1), L0_attn_ln_gamma, L0_attn_ln_beta, L0_attn_w_qkv, L0_attn_w_out, L0_attn_b_out)
    h = h + _L0_ffn_ref(_layernorm(h, axis=-1), L0_ffn_wr, L0_ffn_w1, L0_ffn_b1, L0_ffn_w2, L0_ffn_b2)
    return h

_drawn_inputs = setup_inputs


def setup_inputs(seed=0):
    import zlib

    import numpy as np

    out = dict(_drawn_inputs(seed))
    spreads = {'L0_tok_ln_w': (1.0, 0.2),
     'L0_tok_ln_b': (0.0, 0.1),
     'L0_attn_ln_gamma': (1.0, 0.6),
     'L0_attn_ln_beta': (0.0, 0.543),
     'L0_attn_b_out': (0.0, 0.1),
     'L0_ffn_b1': (0.0, 0.8),
     'L0_ffn_b2': (0.0, 0.8)}
    factors = {'L0_ffn_wr': 6.972, 'L0_ffn_w1': 8.0, 'L0_ffn_w2': 8.0}
    for name, (base, spread) in spreads.items():
        noise = np.random.default_rng([zlib.crc32(name.encode()), seed]).standard_normal(out[name].shape)
        drawn = base * np.exp(spread * noise) if base else spread * noise
        out[name] = jnp.asarray(drawn.astype(out[name].dtype))
    for name, factor in factors.items():
        out[name] = (out[name] * factor).astype(out[name].dtype)
    return out
```

```python
from contextlib import ExitStack

import concourse.bass as bass
from concourse import mybir

F32 = mybir.dt.float32
BF16 = mybir.dt.bfloat16
I32 = mybir.dt.int32
U32 = mybir.dt.uint32
ALU = mybir.AluOpType
ACT = mybir.ActivationFunctionType
AX = mybir.AxisListType

P = 128
IMAGES = 32
IMAGE = 36
TOKENS = IMAGES * IMAGE
PER_GROUP = 3
GROUP = PER_GROUP * IMAGE
GROUPS = -(-TOKENS // GROUP)
LAST = TOKENS - (GROUPS - 1) * GROUP
D = 192
DB = D - P
KB = DB + 1
PATCH = 768
PK = PATCH // P
HEADS = 12
DH = 64
INNER = HEADS * DH
UNITS = 3
UH = HEADS // UNITS
EXPERTS = 16
F = 768
FK = F // P
TOPK = 2
EPS = 1e-5
MASKED = -1e30

WINDOW = 256
WT = WINDOW // P
ROUNDS = -(-TOKENS // WINDOW)
QS = ROUNDS * WT
ROW = EXPERTS * QS
SLOTS = P * ROW
PAIRS = TOPK * TOKENS

FILLS = 5
LOOPED = 2
FIRST_LOOPED = 3


class Group:

    def __init__(self, at, i=None):
        self.no = at if i is None else i * 2 + at
        self.par = at % 2
        self.half = at // 2 if i is None else i + at // 2
        self.live = i is not None or 0 <= at < GROUPS
        self.n = LAST if i is None and at == GROUPS - 1 else GROUP


def due(count):
    return not isinstance(count, int) or count > 0


def held(eng, count):
    return count if isinstance(count, int) else eng.to_reg(count)


def pipeline(eng, iteration):
    for at in range(-2, FIRST_LOOPED):
        iteration(at, None)
    with eng.Fori(0, LOOPED) as i:
        iteration(FIRST_LOOPED, i)
        iteration(FIRST_LOOPED + 1, i)
    for at in range(FIRST_LOOPED + 2 * LOOPED, GROUPS + 1):
        iteration(at, None)


def vit_block(nc, patches, patches_last, tok_w, tok_b, tok_ln_w, tok_ln_b, gamma, beta, w_qkv, w_out, b_out,
              w_router, w1, b1, w2, b2, out):
    z_rows = nc.dram_tensor("z_rows", [TOKENS, D], F32, kind="Internal").ap()
    slot_table = nc.dram_tensor("slot_table", [SLOTS, 1], I32, kind="Internal").ap()
    y_rows = nc.dram_tensor("y_rows", [PAIRS + SLOTS, D], F32, kind="Internal").ap()

    with ExitStack() as ctx:
        def sb(name, shape, dt=F32):
            return ctx.enter_context(nc.sbuf_tensor(name, shape, dt))

        def bank(name, *dims):
            return ctx.enter_context(nc.psum_tensor(name, [P, *(dims or (512,))], F32))

        def sem(name):
            return ctx.enter_context(nc.semaphore(name))

        tokw = sb("tokw", [P, PK, D])
        wqkv_a = sb("wqkv_a", [P, 3 * INNER])
        wqkv_b = sb("wqkv_b", [P, 3 * INNER])
        wo = sb("wo", [P, PK, D])
        wr_a = sb("wr_a", [P, EXPERTS])
        wr_b = sb("wr_b", [P, EXPERTS])
        tokb = sb("tokb", [P, D])
        lnw = sb("lnw", [P, D])
        lnb = sb("lnb", [P, D])
        bo = sb("bo", [P, D])
        gb_a = sb("gb_a", [P, 2])
        gb_b = sb("gb_b", [P, 2])
        b2all = sb("b2all", [P, EXPERTS, D])
        ident = sb("ident", [P, P])
        before = sb("before", [P, P], BF16)
        ones = sb("ones", [P, P], BF16)
        mask_l = sb("mask_l", [P, GROUP], BF16)
        mask_r = sb("mask_r", [P, 2, GROUP], BF16)
        minus_half = sb("minus_half", [P, 1])
        experts = sb("experts", [P, EXPERTS])
        pairs = sb("pairs", [P, GROUPS, TOPK], I32)
        pads = sb("pads", [P, ROW], I32)

        patch = sb("patch", [P, 2, PK * GROUP])
        lin = sb("lin", [P, D])
        lnc = sb("lnc", [P, D])
        h = sb("h", [P, 2, D])
        xc = sb("xc", [P, D])
        st1, st2, st4 = (sb(f"st{k}", [P, 6]) for k in (1, 2, 4))
        mv1, mv2, mv4 = (sb(f"mv{k}", [P, 2]) for k in (1, 2, 4))
        ve1, ve2, ve4 = (sb(f"ve{k}", [P, 1]) for k in (1, 2, 4))
        rs1, rs2, rs4 = (sb(f"rs{k}", [P, 1]) for k in (1, 2, 4))
        hb_all = sb("hb_all", [P, GROUPS, D])
        xn_a = sb("xn_a", [P, 2, GROUP])
        xn_b = sb("xn_b", [P, 2, GROUP])
        qk = sb("qk", [P, 2, UNITS, UH, GROUP])
        v = sb("v", [P, 2, HEADS, DH + 1])
        nmax = sb("nmax", [P, 2, UH])
        prob = sb("prob", [P, 2, UH, GROUP])
        prob_t = sb("prob_t", [P, 2, UH, GROUP])
        rsum = sb("rsum", [P, UH])
        cx = sb("cx", [P, 2, UH, DH])
        cx_t = sb("cx_t", [P, 2, PK, GROUP])
        h2 = sb("h2", [P, 2, D])
        z = sb("z", [P, 2, D])
        zt_a = sb("zt_a", [P, GROUP])
        zt_b = sb("zt_b", [P, GROUP])
        base_all = sb("base_all", [P, GROUPS, D])
        gates_all = sb("gates_all", [P, GROUPS, TOPK])
        top = sb("top", [P, 8])
        top_i = sb("top_i", [P, 8], U32)
        top_e = sb("top_e", [P, TOPK])
        ldiff = sb("ldiff", [P, EXPERTS + TOPK])
        lexp = sb("lexp", [P, EXPERTS + TOPK])
        lsum = sb("lsum", [P, 1])
        lrec = sb("lrec", [P, 1])
        onehot = sb("onehot", [P, TOPK, EXPERTS])
        chosen = sb("chosen", [P, 2, EXPERTS], BF16)
        seen = sb("seen", [P, 2, EXPERTS], BF16)
        rank_e = sb("rank_e", [P, TOPK, EXPERTS])
        rank = sb("rank", [P, TOPK])
        rank_i = sb("rank_i", [P, TOPK], I32)
        block_i = sb("block_i", [P, TOPK], I32)
        rank_w = sb("rank_w", [P, TOPK])
        slot_f = sb("slot_f", [P, TOPK])
        slot = sb("slot", [P, 2, TOPK], I32)
        pair = sb("pair", [P, 2, TOPK], I32)
        most = sb("most", [1, 1])
        most_i = sb("most_i", [1, 1], I32)
        rounds = sb("rounds", [1, 1], I32)
        table = sb("table", [P, ROW], I32)
        table_h = sb("table_h", [P, ROW], I32)
        table_z = sb("table_z", [P, ROW], I32)
        w1_a = sb("w1_a", [P, 2, F])
        w1_b = sb("w1_b", [P, 2, F])
        w2_s = sb("w2_s", [P, 2, FK, D])
        from_row = sb("from_row", [P, 2, WT], I32)
        to_row = sb("to_row", [P, 2, WT], I32)
        zg = sb("zg", [P, 2, WT, D])
        xt_a = sb("xt_a", [P, 2, WINDOW])
        xt_b = sb("xt_b", [P, 2, WINDOW])
        hid = sb("hid", [P, 2, FK, WINDOW])
        y = sb("y", [P, 2, WT, D])
        y_back = sb("y_back", [P, GROUPS, TOPK * D])
        part = sb("part", [P, GROUPS, D])
        result = sb("result", [P, GROUPS, D])

        tok_ps = bank("tok_ps")
        turn_ps = bank("turn_ps")
        fill_ps = [bank("fill0_ps"), bank("fill1_ps")]
        score_ps = bank("score_ps", 2, 512)
        prob_ps = bank("prob_ps")
        ctx_ps = bank("ctx_ps")
        hid_ps = [fill_ps[0], fill_ps[1], prob_ps]

        tokw_in, rows_in, qkv_in, wo_in = sem("tokw_in"), sem("rows_in"), sem("qkv_in"), sem("wo_in")
        patch_in = [sem("patch_in0"), sem("patch_in1")]
        begun = sem("begun")
        const = sem("const")
        pads_made, pads_out = sem("pads_made"), sem("pads_out")
        zeroed = sem("zeroed")
        embed_done, xc_turned, fill_done = sem("embed_done"), sem("xc_turned"), sem("fill_done")
        score_done, prob_turned, av_done = sem("score_done"), sem("prob_turned"), sem("av_done")
        ctx_turned, proj_done, z_turned = sem("ctx_turned"), sem("proj_done"), sem("z_turned")
        logits_done, rank_done, count_done = sem("logits_done"), sem("rank_done"), sem("count_done")
        hid_done, zg_turned, y_done = sem("hid_done"), sem("zg_turned"), sem("y_done")
        xn_ready, fill_read, exp_ready = sem("xn_ready"), sem("fill_read"), sem("exp_ready")
        prob_t_ready, ctx_t_ready, zt_ready = sem("prob_t_ready"), sem("ctx_t_ready"), sem("zt_ready")
        lexp_ready, gelu_ready = sem("lexp_ready"), sem("gelu_ready")
        lin_ready, st1_ready, mv1_ready, lnc_ready, h_ready = (
            sem(s) for s in ("lin_ready", "st1_ready", "mv1_ready", "lnc_ready", "h_ready"))
        st2_ready, mv2_ready, xc_ready = sem("st2_ready"), sem("mv2_ready"), sem("xc_ready")
        max_ready, diff_ready, rsum_ready, ctx_ready = (
            sem(s) for s in ("max_ready", "diff_ready", "rsum_ready", "ctx_ready"))
        h2_ready, st4_ready, mv4_ready, z_ready = (
            sem(s) for s in ("h2_ready", "st4_ready", "mv4_ready", "z_ready"))
        top_ready, top_i_ready, top_e_ready, ldiff_ready = (
            sem(s) for s in ("top_ready", "top_i_ready", "top_e_ready", "ldiff_ready"))
        lsum_ready, lrec_ready, gates_ready = sem("lsum_ready"), sem("lrec_ready"), sem("gates_ready")
        onehot_ready, chosen_ready, seen_ready = sem("onehot_ready"), sem("chosen_ready"), sem("seen_ready")
        rank_ready, rank_i_ready, block_ready, slot_f_ready, slot_ready = (
            sem(s) for s in ("rank_ready", "rank_i_ready", "block_ready", "slot_f_ready", "slot_ready"))
        most_ready, most_i_ready, rounds_ready = sem("most_ready"), sem("most_i_ready"), sem("rounds_ready")
        halved, rows_ready = sem("halved"), sem("rows_ready")
        xt_ready, y_ready = sem("xt_ready"), sem("y_ready")
        part_ready, result_ready = sem("part_ready"), sem("result_ready")
        ve1_ready, rs1_ready, ve2_ready, rs2_ready, ve4_ready, rs4_ready = (
            sem(s) for s in ("ve1_ready", "rs1_ready", "ve2_ready", "rs2_ready", "ve4_ready", "rs4_ready"))
        hb_ready, base_ready, pair_ready = sem("hb_ready"), sem("base_ready"), sem("pair_ready")
        from_ready, to_ready = sem("from_ready"), sem("to_ready")
        z_out = [sem("z_out0"), sem("z_out1")]
        slots_out = [sem("slots_out0"), sem("slots_out1")]
        table_in = sem("table_in")
        w_in = [sem("w_in0"), sem("w_in1")]
        zg_in = [sem("zg_in0"), sem("zg_in1")]
        y_out = [sem("y_out0"), sem("y_out1")]
        y_in = sem("y_in")
        all_out = sem("all_out")

        W_DMAS = 4
        CONSTS = 6
        Y0 = 2
        GELU0 = 3
        HID0 = 1
        TO0 = 1

        def unit_of(g, u):
            return UNITS * g.no + u, (g.par + u) % 2

        def scores_view(n):
            return score_ps[0:n, :, 0:2 * GROUP].rearrange("p e (j s) -> p e j s", j=2)[:, :, :, 0:n]

        def prob_view(tile, buf, n):
            return tile[0:n, buf, :, 0:n].rearrange("p (e j) s -> p e j s", e=2)

        block = ctx.enter_context(nc.Block())

        @block.sync
        def _(sp):
            def load_patches(a):
                count = held(sp, a.no - 1)
                sp.wait_ge(begun, 1)
                if due(count):
                    sp.wait_ge(embed_done, count)
                dst = patch[:, a.par, 0:PK * a.n]
                src = patches_last if a.n == LAST else patches[bass.ds(a.no, 1)].rearrange("a p n -> (a p) n")
                sp.dma_start(dst, src).then_inc(patch_in[a.par], 16)

            sp.dma_start(tokw[:, :, :], tok_w.rearrange("p (k n) -> p k n", k=PK)).then_inc(tokw_in, 16)
            load_patches(Group(0))
            for tile, row in ((tokb, tok_b), (lnw, tok_ln_w), (lnb, tok_ln_b), (bo, b_out)):
                sp.dma_start(tile[:, :], row.rearrange("(a n) -> a n", a=1).to_broadcast([P, D])).then_inc(rows_in, 16)
            for c, col in enumerate((gamma, beta)):
                column = col.rearrange("(n a) -> n a", a=1)
                sp.dma_start(gb_a[:, c:c + 1], column[0:P, :]).then_inc(rows_in, 16)
                sp.dma_start(gb_b[0:DB, c:c + 1], column[P:D, :]).then_inc(rows_in, 16)
            load_patches(Group(1))
            sp.dma_start(wqkv_a[:, :], w_qkv[0:P, :]).then_inc(qkv_in, 16)
            sp.dma_start(wqkv_b[0:DB, :], w_qkv[P:D, :]).then_inc(qkv_in, 16)
            sp.dma_start(wo[:, :, :], w_out.rearrange("p (k n) -> p k n", k=PK)).then_inc(wo_in, 16)
            sp.dma_start(wr_a[:, :], w_router[0:P, :]).then_inc(wo_in, 16)
            sp.dma_start(wr_b[0:DB, :], w_router[P:D, :]).then_inc(wo_in, 16)
            sp.wait_ge(pads_made, 1)
            sp.dma_start(slot_table.rearrange("(p s) a -> p (s a)", p=P), pads[:, :]).then_inc(pads_out, 16)
            sp.dma_start(b2all[:, :, :], b2.rearrange("e n -> (e n)").rearrange("(a n) -> a n", a=1)
                         .to_broadcast([P, EXPERTS * D]).rearrange("p (e n) -> p e n", e=EXPERTS)).then_inc(rows_in, 16)

            def iteration(at, i):
                d, a = Group(at - 1, i), Group(at + 2, i)
                if a.live and at >= 0:
                    load_patches(a)
                if d.live:
                    sp.wait_ge(z_ready, d.no + 1)
                    sp.dma_start(z_rows[bass.ds(d.no * GROUP, d.n), :], z[0:d.n, d.par, :]).then_inc(z_out[d.par], 16)

            pipeline(sp, iteration)

            def load_expert(buf, e, n):
                if not isinstance(n, int):
                    sp.wait_ge(y_done, n - 1 + Y0)
                one = bass.ds(e, 1)
                sp.dma_start(w1_a[:, buf, :], w1[one, 0:P, :].rearrange("a p n -> (a p) n")).then_inc(w_in[buf], 16)
                sp.dma_start(w1_b[0:DB, buf, :], w1[one, P:D, :].rearrange("a p n -> (a p) n")).then_inc(w_in[buf], 16)
                sp.dma_start(w1_b[DB:KB, buf, :], b1[one, :]).then_inc(w_in[buf], 16)
                sp.dma_start(w2_s[:, buf, :, :], w2[one].rearrange("a p (k n) -> (a p) k n", k=FK)).then_inc(w_in[buf], 16)

            load_expert(0, 0, 0)
            load_expert(1, 1, 1)
            for buf in range(2):
                sp.wait_ge(slots_out[buf], 16 * TOPK * ((GROUPS + 1 - buf) // 2))
            sp.dma_start(table[:, :], slot_table.rearrange("(p s) a -> p (s a)", p=P)).then_inc(table_in, 16)
            sp.wait_ge(rounds_ready, 1)
            with sp.Fori(0, sp.value_load(rounds[0:1, 0:1], min_val=1, max_val=ROUNDS)) as r:
                with sp.Fori(0, EXPERTS // 2 - 1) as j:
                    for buf in range(2):
                        load_expert(buf, j * 2 + (2 + buf), r * EXPERTS + j * 2 + (2 + buf))
                for buf in range(2):
                    load_expert(buf, buf, r * EXPERTS + (EXPERTS + buf))
            steps = sp.value_load(rounds[0:1, 0:1], min_val=1, max_val=ROUNDS) * (EXPERTS // 2)
            for buf in range(2):
                count, count_free = held(sp, steps * (16 * W_DMAS) + 16 * W_DMAS), held(sp, steps * (16 * WT))
                sp.wait_ge(begun, 1)
                sp.wait_ge(w_in[buf], count)
                sp.wait_ge(y_out[buf], count_free)
            G1 = GROUPS - 1
            rows = y_rows[0:PAIRS, :].rearrange("(t k) n -> t (k n)", k=TOPK)
            sp.dma_start(y_back[0:GROUP, 0:G1, :], rows[0:G1 * GROUP, :].rearrange("(g t) n -> t g n", g=G1)).then_inc(y_in, 16)
            sp.dma_start(y_back[0:LAST, G1, :], rows[G1 * GROUP:, :]).then_inc(y_in, 16)
            sp.wait_ge(result_ready, GROUPS)
            sp.dma_start(out[0:G1 * GROUP, :].rearrange("(g t) n -> t g n", g=G1), result[0:GROUP, 0:G1, :]).then_inc(all_out, 16)
            sp.dma_start(out[G1 * GROUP:, :], result[0:LAST, G1, :]).then_inc(all_out, 16)
            sp.wait_ge(all_out, 32)

        @block.gpsimd
        def _(pool):
            pool.memset(ident[:, :], 0.0).then_inc(begun, 1)
            pool.memset(before[:, :], 1.0).then_inc(zeroed, 1)
            pool.memset(mask_l[:, :], 1.0).then_inc(zeroed, 1)
            pool.memset(mask_r[:, :, :], 0.0).then_inc(zeroed, 1)
            pool.memset(ones[:, :], 1.0).then_inc(const, 1)
            pool.memset(minus_half[:, :], -0.5).then_inc(const, 1)
            pool.wait_ge(begun, 1)
            pool.wait_ge(zeroed, 3)
            pool.affine_select(out=ident[:, :], in_=ident[:, :], compare_op=ALU.not_equal, fill=1.0,
                               base=0, pattern=[[-1, P]], channel_multiplier=1).then_inc(const, 1)
            pool.affine_select(out=before[:, :], in_=before[:, :], compare_op=ALU.is_gt, fill=0.0,
                               base=0, pattern=[[1, P]], channel_multiplier=-1).then_inc(const, 1)
            pool.affine_select(out=mask_l[:, :], in_=mask_l[:, :], compare_op=ALU.is_ge, fill=0.0,
                               base=0, pattern=[[1, GROUP]], channel_multiplier=-IMAGE).then_inc(zeroed, 1)
            pool.affine_select(out=mask_r[:, :, :], in_=mask_r[:, :, :], compare_op=ALU.is_ge, fill=MASKED,
                               base=0, pattern=[[0, 2], [1, GROUP]], channel_multiplier=-IMAGE).then_inc(zeroed, 1)
            pool.wait_ge(zeroed, 5)
            pool.affine_select(out=mask_l[:, :], in_=mask_l[:, :], compare_op=ALU.is_ge, fill=0.0,
                               base=IMAGE - 1, pattern=[[-1, GROUP]], channel_multiplier=IMAGE).then_inc(const, 1)
            pool.affine_select(out=mask_r[:, :, :], in_=mask_r[:, :, :], compare_op=ALU.is_ge, fill=MASKED,
                               base=IMAGE - 1, pattern=[[0, 2], [-1, GROUP]], channel_multiplier=IMAGE).then_inc(const, 1)
            pool.iota(pads[:, :], pattern=[[1, ROW]], base=PAIRS, channel_multiplier=ROW).then_inc(pads_made, 1)
            pool.iota(pairs[:, :, :], pattern=[[TOPK * GROUP, GROUPS], [1, TOPK]], base=0,
                      channel_multiplier=TOPK).then_inc(pads_made, 1)
            pool.wait_ge(pads_made, 2)

            def rsqrt(n, mv, scale, shift, ve, ve_ready, rs, rs_ready, no):
                pool.tensor_scalar(ve[0:n, :], mv[0:n, 1:2], scale, shift, ALU.mult, ALU.add).then_inc(ve_ready, 1)
                pool.wait_ge(ve_ready, no + 1)
                pool.tensor_tensor(rs[0:n, :], ve[0:n, :], minus_half[0:n, :], ALU.pow).then_inc(rs_ready, 1)

            def iteration(at, i):
                d, a = Group(at - 1, i), Group(at + 2, i)
                if d.live:
                    count, count_free = held(pool, d.no + 1), held(pool, d.no)
                    pool.wait_ge(begun, 1)
                    pool.wait_ge(mv4_ready, count)
                    if due(count_free):
                        pool.wait_ge(z_ready, count_free)
                    rsqrt(d.n, mv4, 1.0, EPS, ve4, ve4_ready, rs4, rs4_ready, d.no)
                if a.live:
                    count, count_free = held(pool, a.no + 1), held(pool, a.no)
                    pool.wait_ge(begun, 1)
                    pool.wait_ge(mv1_ready, count)
                    if due(count_free):
                        pool.wait_ge(h_ready, count_free)
                    rsqrt(a.n, mv1, 1.0, EPS, ve1, ve1_ready, rs1, rs1_ready, a.no)
                    count, count_free = held(pool, a.no + 1), held(pool, a.no)
                    pool.wait_ge(begun, 1)
                    pool.wait_ge(mv2_ready, count)
                    if due(count_free):
                        pool.wait_ge(xc_ready, count_free)
                    rsqrt(a.n, mv2, 1.0 + EPS, EPS * EPS, ve2, ve2_ready, rs2, rs2_ready, a.no)
                    if at == -2:
                        pool.wait_ge(rows_in, 16 * 9)
                    pool.tensor_tensor(hb_all[0:a.n, bass.ds(a.no, 1), :].rearrange("p a n -> p (a n)"),
                                       h[0:a.n, a.par, :], bo[0:a.n, :], ALU.add).then_inc(hb_ready, 1)
                if d.live:
                    pool.wait_ge(z_ready, d.no + 1)
                    pool.tensor_tensor(base_all[0:d.n, bass.ds(d.no, 1), :].rearrange("p a n -> p (a n)"),
                                       h2[0:d.n, d.par, :], z[0:d.n, d.par, :], ALU.add).then_inc(base_ready, 1)
                    if due(d.half * (16 * TOPK)):
                        pool.wait_ge(slots_out[d.par], d.half * (16 * TOPK))
                    pool.tensor_copy(pair[0:d.n, d.par, :],
                                     pairs[0:d.n, bass.ds(d.no, 1), :].rearrange("p a n -> p (a n)")).then_inc(pair_ready, 1)
                    count, count_free = held(pool, d.no + 1), held(pool, d.no + 1)
                    pool.wait_ge(begun, 1)
                    pool.wait_ge(pair_ready, count)
                    pool.wait_ge(slot_ready, count_free)
                    if at == 1:
                        pool.wait_ge(pads_out, 16)
                    for k in range(TOPK):
                        pool.indirect_dma_start(
                            slot_table, bass.IndirectOffsetOnAxis(ap=slot[0:d.n, d.par, k:k + 1], axis=0),
                            pair[0:d.n, d.par, k:k + 1], None).then_inc(slots_out[d.par], 16)

            pipeline(pool, iteration)

            def gather(buf, col, n):
                pool.tensor_copy(from_row[:, buf, :], table_z[:, bass.ds(col, WT)]).then_inc(from_ready, 1)
                count = held(pool, n + 1)
                pool.wait_ge(begun, 1)
                pool.wait_ge(from_ready, count)
                for t in range(WT):
                    pool.indirect_dma_start(
                        zg[:, buf, t, :], None, z_rows,
                        bass.IndirectOffsetOnAxis(ap=from_row[:, buf, t:t + 1], axis=0)).then_inc(zg_in[buf], 16)

            pool.sem_inc(to_ready, TO0)
            pool.wait_ge(rows_ready, 1)
            for buf in range(2):
                pool.wait_ge(z_out[buf], 16 * ((GROUPS + 1 - buf) // 2))
            gather(0, 0, 0)
            gather(1, QS, 1)
            pool.tensor_copy(to_row[:, 0, :], table[:, 0:WT]).then_inc(to_ready, 1)
            pool.wait_ge(rounds_ready, 1)
            with pool.Fori(0, pool.value_load(rounds[0:1, 0:1], min_val=1, max_val=ROUNDS)) as r:
                def pair_of_experts(j, last):
                    half = r * (EXPERTS // 2) + j
                    for buf in range(2):
                        n = r * EXPERTS + j * 2 + buf
                        pool.wait_ge(zg_in[buf], half * (16 * WT) + 16 * WT)
                        pool.wait_ge(zg_turned, n + 1)
                        gather(buf, r * WT + (WT + buf * QS) if last else j * (2 * QS) + ((2 + buf) * QS) + r * WT, n + 2)
                        count, count_y = held(pool, n + (1 + TO0)), held(pool, n + (1 + Y0))
                        pool.wait_ge(begun, 1)
                        pool.wait_ge(to_ready, count)
                        pool.wait_ge(y_ready, count_y)
                        for t in range(WT):
                            pool.indirect_dma_start(
                                y_rows, bass.IndirectOffsetOnAxis(ap=to_row[:, buf, t:t + 1], axis=0),
                                y[:, buf, t, :], None).then_inc(y_out[buf], 16)
                        pool.wait_ge(y_out[buf], half * (16 * WT) + 16 * WT)
                        pool.tensor_copy(to_row[:, 1 - buf, :],
                                         table[:, bass.ds(r * WT + WT if last and buf else j * (2 * QS) + (1 + buf) * QS + r * WT, WT)]
                                         ).then_inc(to_ready, 1)

                with pool.Fori(0, EXPERTS // 2 - 1) as j:
                    pair_of_experts(j, False)
                pair_of_experts(EXPERTS // 2 - 1, True)
            halves = pool.value_load(rounds[0:1, 0:1], min_val=1, max_val=ROUNDS) * (EXPERTS // 2)
            for buf in range(2):
                pool.wait_ge(zg_in[buf], halves * (16 * WT) + 16 * WT)

        @block.scalar
        def _(act):
            def turn_xn(a):
                act.wait_ge(xc_turned, a.no + 1)
                if due(a.no * FILLS - FILLS):
                    act.wait_ge(fill_done, a.no * FILLS - FILLS)
                act.activation(xn_a[:, a.par, 0:a.n], turn_ps[:, 0:a.n], ACT.Identity,
                               bias=gb_a[:, 1:2], scale=gb_a[:, 0:1])
                act.activation(xn_b[0:DB, a.par, 0:a.n], turn_ps[0:DB, P:P + a.n], ACT.Identity,
                               bias=gb_b[0:DB, 1:2], scale=gb_b[0:DB, 0:1]).then_inc(xn_ready, 1)

            def read_fill(b, f):
                ps = fill_ps[(b.par + f) % 2]
                act.wait_ge(fill_done, b.no * FILLS + (f + 1))
                if f < UNITS:
                    if due(b.no * UNITS + (f + 1 - 2 * UNITS)):
                        act.wait_ge(score_done, b.no * UNITS + (f + 1 - 2 * UNITS))
                    act.activation(qk[:, b.par, f, :, 0:b.n],
                                   ps[:, 0:UH * GROUP].rearrange("p (c t) -> p c t", c=UH)[:, :, 0:b.n],
                                   ACT.Copy).then_inc(fill_read, 1)
                else:
                    half = HEADS // 2
                    if due(b.no * UNITS + (UNITS - 2 * UNITS)):
                        act.wait_ge(av_done, b.no * UNITS + (UNITS - 2 * UNITS))
                    act.activation(v[0:b.n, b.par, (f - UNITS) * half:(f - UNITS + 1) * half, 0:DH],
                                   ps[0:b.n, 0:half * DH].rearrange("p (c t) -> p c t", c=half),
                                   ACT.Copy).then_inc(fill_read, 1)

            def exp(g, u):
                no, buf = unit_of(g, u)
                act.wait_ge(diff_ready, no + 1)
                act.activation(prob[0:g.n, buf, :, 0:g.n], prob[0:g.n, buf, :, 0:g.n], ACT.Exp,
                               scale=DH ** -0.5).then_inc(exp_ready, 1)

            def turn_prob(g, u):
                no, buf = unit_of(g, u)
                act.wait_ge(prob_turned, no + 1)
                if due(no - 1):
                    act.wait_ge(av_done, no - 1)
                act.activation(prob_t[0:g.n, buf, :, 0:g.n],
                               prob_ps[0:g.n, 0:UH * GROUP].rearrange("p (c t) -> p c t", c=UH)[:, :, 0:g.n],
                               ACT.Copy).then_inc(prob_t_ready, 1)

            def turn_ctx(g, u):
                no, _ = unit_of(g, u)
                act.wait_ge(ctx_turned, no + 1)
                if due(g.no - 1):
                    act.wait_ge(proj_done, g.no - 1)
                act.activation(cx_t[:, g.par, 2 * u:2 * u + 2, 0:g.n],
                               ctx_ps[:, UH * (DH + 1):UH * (DH + 1) + 2 * GROUP]
                               .rearrange("p (c t) -> p c t", c=2)[:, :, 0:g.n], ACT.Copy).then_inc(ctx_t_ready, 1)

            def turn_z(d):
                act.wait_ge(z_turned, d.no + 1)
                if due(d.no):
                    act.wait_ge(logits_done, d.no)
                act.activation(zt_a[:, 0:d.n], turn_ps[:, 0:d.n], ACT.Copy)
                act.activation(zt_b[0:DB, 0:d.n], turn_ps[0:DB, P:P + d.n], ACT.Copy).then_inc(zt_ready, 1)

            def router_exp(d):
                act.wait_ge(ldiff_ready, d.no + 1)
                if due(d.no):
                    act.wait_ge(gates_ready, d.no)
                act.activation(lexp[0:d.n, :], ldiff[0:d.n, :], ACT.Exp).then_inc(lexp_ready, 1)

            def iteration(at, i):
                g, d, b, a = (Group(at + k, i) for k in (0, -1, 1, 2))
                if g.live:
                    exp(g, 0)
                if b.live:
                    read_fill(b, 0)
                if d.live:
                    turn_z(d)
                if g.live:
                    turn_prob(g, 0)
                    exp(g, 1)
                if d.live:
                    router_exp(d)
                if b.live:
                    read_fill(b, 1)
                if g.live:
                    turn_prob(g, 1)
                    turn_ctx(g, 0)
                    exp(g, 2)
                if b.live:
                    read_fill(b, 2)
                if g.live:
                    turn_prob(g, 2)
                if b.live:
                    read_fill(b, 3)
                if g.live:
                    turn_ctx(g, 1)
                if a.live:
                    turn_xn(a)
                if b.live:
                    read_fill(b, 4)
                if g.live:
                    turn_ctx(g, 2)

            act.wait_ge(rows_in, 16 * 9)
            pipeline(act, iteration)

            act.sem_inc(gelu_ready, GELU0)
            act.wait_ge(rounds_ready, 1)
            with act.Fori(0, act.value_load(rounds[0:1, 0:1], min_val=1, max_val=ROUNDS)) as r:
                with act.Fori(0, EXPERTS // 2) as j:
                    for buf in range(2):
                        n = r * EXPERTS + j * 2 + buf
                        act.wait_ge(y_done, n - 1 + Y0)
                        for c in range(FK // 2):
                            act.wait_ge(hid_done, n * 3 + (c + 1 + HID0))
                            act.activation(hid[:, buf, 2 * c:2 * c + 2, :],
                                           hid_ps[c][:, :].rearrange("p (k t) -> p k t", k=2),
                                           ACT.Gelu).then_inc(gelu_ready, 1)

        @block.vector
        def _(dve):
            dve.memset(v[:, :, :, DH:DH + 1], 1.0).then_inc(const, 1)
            for tile in (xn_b, xt_b):
                for buf in range(2):
                    dve.memset(tile[DB:KB, buf, :], 0.0 if tile is xn_b else 1.0).then_inc(const, 1)
            dve.memset(zt_b[DB:KB, :], 0.0).then_inc(const, 1)
            dve.memset(wqkv_b[DB:KB, :], 0.0).then_inc(const, 1)
            dve.memset(wr_b[DB:KB, :], 0.0).then_inc(const, 1)
            dve.memset(seen[:, :, :], 0.0).then_inc(const, 1)
            dve.memset(experts[:, :], 0.0).then_inc(const, 1)

            def embed_stats(a):
                dve.wait_ge(embed_done, a.no + 1)
                dve.tensor_tensor(lin[0:a.n, :], tok_ps[0:a.n, 0:D], tokb[0:a.n, :], ALU.add).then_inc(lin_ready, 1)
                dve.wait_ge(lin_ready, a.no + 1)
                dve.bn_stats(st1[0:a.n, :], lin[0:a.n, :]).then_inc(st1_ready, 1)
                count = held(dve, a.no + 1)
                dve.wait_ge(begun, 1)
                dve.wait_ge(st1_ready, count)
                dve.bn_aggr(mv1[0:a.n, :], st1[0:a.n, :]).then_inc(mv1_ready, 1)

            def embed_norm(a):
                dve.wait_ge(mv1_ready, a.no + 1)
                dve.scalar_tensor_tensor(lnc[0:a.n, :], lin[0:a.n, :], mv1[0:a.n, 0:1], lnw[0:a.n, :],
                                         ALU.subtract, ALU.mult).then_inc(lnc_ready, 1)
                dve.wait_ge(lnc_ready, a.no + 1)
                dve.wait_ge(rs1_ready, a.no + 1)
                if due(a.no - 1):
                    dve.wait_ge(hb_ready, a.no - 1)
                dve.scalar_tensor_tensor(h[0:a.n, a.par, :], lnc[0:a.n, :], rs1[0:a.n, :], lnb[0:a.n, :],
                                         ALU.mult, ALU.add).then_inc(h_ready, 1)
                dve.wait_ge(h_ready, a.no + 1)
                dve.bn_stats(st2[0:a.n, :], h[0:a.n, a.par, :]).then_inc(st2_ready, 1)
                count = held(dve, a.no + 1)
                dve.wait_ge(begun, 1)
                dve.wait_ge(st2_ready, count)
                dve.bn_aggr(mv2[0:a.n, :], st2[0:a.n, :]).then_inc(mv2_ready, 1)

            def centre(a):
                dve.wait_ge(mv2_ready, a.no + 1)
                dve.wait_ge(rs2_ready, a.no + 1)
                if due(a.no):
                    dve.wait_ge(xc_turned, a.no)
                dve.tensor_scalar(xc[0:a.n, :], h[0:a.n, a.par, :], mv2[0:a.n, 0:1], rs2[0:a.n, :],
                                  ALU.subtract, ALU.mult).then_inc(xc_ready, 1)

            def scores_less_max(g, u):
                no, buf = unit_of(g, u)
                dve.wait_ge(score_done, no + 1)
                dve.tensor_reduce(nmax[0:g.n, buf, :].rearrange("p (e j) -> p e j", e=2), scores_view(g.n), AX.X, ALU.max,
                                  negate=True).then_inc(max_ready, 1)
                dve.wait_ge(max_ready, no + 1)
                if due(no - 1):
                    dve.wait_ge(prob_turned, no - 1)
                dve.tensor_tensor(prob_view(prob, buf, g.n), scores_view(g.n),
                                  nmax[0:g.n, buf, :].rearrange("p (e j) -> p e j", e=2).unsqueeze(3)
                                  .to_broadcast([g.n, 2, 2, g.n]), ALU.add).then_inc(diff_ready, 1)

            def context(g, u):
                no, buf = unit_of(g, u)
                both = ctx_ps[0:g.n, 0:UH * (DH + 1)].rearrange("p (c t) -> p c t", c=UH)
                dve.wait_ge(av_done, no + 1)
                dve.reciprocal(rsum[0:g.n, :].unsqueeze(2), both[:, :, DH:DH + 1]).then_inc(rsum_ready, 1)
                dve.wait_ge(rsum_ready, no + 1)
                if due(no - 1):
                    dve.wait_ge(ctx_turned, no - 1)
                dve.tensor_tensor(cx[0:g.n, buf, :, :], both[:, :, 0:DH],
                                  rsum[0:g.n, :].unsqueeze(2).to_broadcast([g.n, UH, DH]),
                                  ALU.mult).then_inc(ctx_ready, 1)

            def residual(d):
                dve.wait_ge(proj_done, d.no + 1)
                dve.wait_ge(hb_ready, d.no + 1)
                if due(d.no - 1):
                    dve.wait_ge(base_ready, d.no - 1)
                dve.tensor_tensor(h2[0:d.n, d.par, :], tok_ps[0:d.n, 0:D],
                                  hb_all[0:d.n, bass.ds(d.no, 1), :].rearrange("p a n -> p (a n)"),
                                  ALU.add).then_inc(h2_ready, 1)
                dve.wait_ge(h2_ready, d.no + 1)
                dve.bn_stats(st4[0:d.n, :], h2[0:d.n, d.par, :]).then_inc(st4_ready, 1)
                count = held(dve, d.no + 1)
                dve.wait_ge(begun, 1)
                dve.wait_ge(st4_ready, count)
                dve.bn_aggr(mv4[0:d.n, :], st4[0:d.n, :]).then_inc(mv4_ready, 1)

            def norm_z(d):
                dve.wait_ge(mv4_ready, d.no + 1)
                dve.wait_ge(rs4_ready, d.no + 1)
                if due(d.no - 1):
                    dve.wait_ge(z_turned, d.no - 1)
                if due(d.half * 16):
                    dve.wait_ge(z_out[d.par], d.half * 16)
                dve.tensor_scalar(z[0:d.n, d.par, :], h2[0:d.n, d.par, :], mv4[0:d.n, 0:1], rs4[0:d.n, :],
                                  ALU.subtract, ALU.mult).then_inc(z_ready, 1)

            def choose(d):
                n, logits = d.n, turn_ps[0:d.n, 256:256 + EXPERTS]
                count = held(dve, d.no + 1)
                dve.wait_ge(begun, 1)
                dve.wait_ge(logits_done, count)
                dve.max(top[0:n, :], logits).then_inc(top_ready, 1)
                count = held(dve, d.no + 1)
                dve.wait_ge(begun, 1)
                dve.wait_ge(top_ready, count)
                dve.max_index(top_i[0:n, :], top[0:n, :], logits).then_inc(top_i_ready, 1)
                dve.tensor_scalar(ldiff[0:n, 0:EXPERTS], logits, top[0:n, 0:1], None, ALU.subtract)
                dve.tensor_scalar(ldiff[0:n, EXPERTS:], top[0:n, 0:TOPK], top[0:n, 0:1], None,
                                  ALU.subtract).then_inc(ldiff_ready, 1)
                dve.wait_ge(top_i_ready, d.no + 1)
                dve.tensor_copy(top_e[0:n, :], top_i[0:n, 0:TOPK]).then_inc(top_e_ready, 1)
                dve.wait_ge(top_e_ready, d.no + 1)
                for k in range(TOPK):
                    op = dve.tensor_scalar(onehot[0:n, k, :], experts[0:n, :], top_e[0:n, k:k + 1], None, ALU.is_equal)
                op.then_inc(onehot_ready, 1)
                dve.wait_ge(onehot_ready, d.no + 1)
                if due(d.no - 1):
                    dve.wait_ge(rank_done, d.no - 1)
                dve.tensor_tensor(chosen[0:n, d.par, :], onehot[0:n, 0, :], onehot[0:n, 1, :], ALU.add).then_inc(chosen_ready, 1)
                dve.wait_ge(chosen_ready, d.no + 1)
                if due(d.no):
                    dve.wait_ge(seen_ready, d.no)
                if due(d.no):
                    dve.wait_ge(rank_done, d.no)
                dve.tensor_tensor(seen[0:n, 1 - d.par, :], seen[0:n, d.par, :], chosen[0:n, d.par, :],
                                  ALU.add).then_inc(seen_ready, 1)

            def gates(d):
                dve.wait_ge(lexp_ready, d.no + 1)
                dve.tensor_reduce(lsum[0:d.n, :], lexp[0:d.n, 0:EXPERTS], AX.X, ALU.add).then_inc(lsum_ready, 1)
                dve.wait_ge(lsum_ready, d.no + 1)
                dve.reciprocal(lrec[0:d.n, :], lsum[0:d.n, :]).then_inc(lrec_ready, 1)
                dve.wait_ge(lrec_ready, d.no + 1)
                dve.tensor_scalar(gates_all[0:d.n, bass.ds(d.no, 1), :].rearrange("p a n -> p (a n)"),
                                  lexp[0:d.n, EXPERTS:], lrec[0:d.n, :], None, ALU.mult).then_inc(gates_ready, 1)

            def slots(d):
                n = d.n
                dve.wait_ge(rank_done, d.no + 1)
                if due(d.no):
                    dve.wait_ge(rank_ready, d.no)
                dve.tensor_tensor(rank_e[0:n, :, :], onehot[0:n, :, :],
                                  turn_ps[0:n, 288:288 + EXPERTS].unsqueeze(1).to_broadcast([n, TOPK, EXPERTS]),
                                  ALU.mult).then_inc(rank_ready, 1)
                dve.wait_ge(rank_ready, d.no + 1)
                dve.tensor_reduce(rank[0:n, :], rank_e[0:n, :, :], AX.X, ALU.add).then_inc(rank_i_ready, 1)
                dve.wait_ge(rank_i_ready, d.no * 2 + 1)
                dve.tensor_copy(rank_i[0:n, :], rank[0:n, :]).then_inc(rank_i_ready, 1)
                dve.wait_ge(rank_i_ready, d.no * 2 + 2)
                dve.tensor_scalar(block_i[0:n, :], rank_i[0:n, :], 7, None, ALU.logical_shift_right).then_inc(block_ready, 1)
                dve.tensor_scalar(rank_w[0:n, :], rank[0:n, :], float(ROW), None, ALU.mult).then_inc(slot_f_ready, 1)
                dve.wait_ge(slot_f_ready, d.no * 2 + 1)
                dve.scalar_tensor_tensor(slot_f[0:n, :], top_e[0:n, :], float(QS), rank_w[0:n, :], ALU.mult,
                                         ALU.add).then_inc(slot_f_ready, 1)
                dve.wait_ge(block_ready, d.no + 1)
                dve.wait_ge(slot_f_ready, d.no * 2 + 2)
                if due(d.half * (16 * TOPK)):
                    dve.wait_ge(slots_out[d.par], d.half * (16 * TOPK))
                dve.scalar_tensor_tensor(slot[0:n, d.par, :], block_i[0:n, :], float(1 - P * ROW), slot_f[0:n, :],
                                         ALU.mult, ALU.add).then_inc(slot_ready, 1)

            def iteration(at, i):
                g, d, a = (Group(at + k, i) for k in (0, -1, 2))
                if d.live:
                    residual(d)
                if g.live:
                    scores_less_max(g, 0)
                if d.live:
                    norm_z(d)
                if g.live:
                    scores_less_max(g, 1)
                if a.live:
                    embed_stats(a)
                if d.live:
                    choose(d)
                if g.live:
                    context(g, 0)
                if a.live:
                    embed_norm(a)
                if g.live:
                    scores_less_max(g, 2)
                if d.live:
                    gates(d)
                if a.live:
                    centre(a)
                if g.live:
                    context(g, 1)
                if d.live:
                    slots(d)
                if g.live:
                    context(g, 2)

            for e in range(1, EXPERTS):
                if e == 1:
                    dve.wait_ge(const, CONSTS + 10)
                op = dve.memset(experts[:, e:e + 1], float(e))
            op.then_inc(const, 1)
            dve.wait_ge(const, CONSTS + 11)
            dve.wait_ge(rows_in, 16 * 9)
            pipeline(dve, iteration)

            dve.wait_ge(count_done, 1)
            dve.tensor_reduce(most[:, :], tok_ps[0:1, 256:256 + EXPERTS], AX.X, ALU.max).then_inc(most_ready, 1)
            dve.wait_ge(most_ready, 1)
            dve.tensor_scalar(most_i[:, :], most[:, :], float(WINDOW - 1), None, ALU.add).then_inc(most_i_ready, 1)
            dve.wait_ge(most_i_ready, 1)
            dve.tensor_scalar(rounds[:, :], most_i[:, :], 8, None, ALU.logical_shift_right).then_inc(rounds_ready, 1)
            dve.wait_ge(table_in, 16)
            dve.tensor_scalar(table_h[:, :], table[:, :], 1, None, ALU.logical_shift_right).then_inc(halved, 1)
            dve.wait_ge(halved, 1)
            dve.tensor_scalar(table_z[:, :], table_h[:, :], float(TOKENS - 1), None, ALU.min).then_inc(rows_ready, 1)

            def turned(buf, steps, before_last=0):
                dve.wait_ge(zg_turned, steps + 1)
                if not isinstance(steps, int):
                    dve.wait_ge(hid_done, before_last * 3 + HID0)
                dve.tensor_copy(xt_a[:, buf, :], turn_ps[:, 0:WINDOW])
                dve.tensor_copy(xt_b[0:DB, buf, :], turn_ps[0:DB, WINDOW:2 * WINDOW]).then_inc(xt_ready, 1)

            turned(0, 0)
            dve.sem_inc(y_ready, Y0)
            dve.wait_ge(rounds_ready, 1)
            with dve.Fori(0, dve.value_load(rounds[0:1, 0:1], min_val=1, max_val=ROUNDS)) as r:
                with dve.Fori(0, EXPERTS // 2) as j:
                    for buf in range(2):
                        n = r * EXPERTS + j * 2 + buf
                        turned(1 - buf, n + 1, n)
                        dve.wait_ge(y_done, n + 1 + Y0)
                        dve.wait_ge(to_ready, n + TO0)
                        dve.tensor_tensor(y[:, buf, :, :],
                                          score_ps[:, buf, 0:WT * D].rearrange("p (t n) -> p t n", t=WT),
                                          b2all[:, bass.ds(j * 2 + buf, 1), :].to_broadcast([P, WT, D]),
                                          ALU.add).then_inc(y_ready, 1)

            dve.wait_ge(y_in, 32)
            dve.wait_ge(base_ready, GROUPS)
            for at in range(GROUPS):
                n = Group(at).n
                dve.scalar_tensor_tensor(part[0:n, at, :], y_back[0:n, at, 0:D], gates_all[0:n, at, 0:1],
                                         base_all[0:n, at, :], ALU.mult, ALU.add).then_inc(part_ready, 1)
                dve.wait_ge(part_ready, at + 1)
                dve.scalar_tensor_tensor(result[0:n, at, :], y_back[0:n, at, D:2 * D], gates_all[0:n, at, 1:2],
                                         part[0:n, at, :], ALU.mult, ALU.add).then_inc(result_ready, 1)

        @block.tensor
        def _(pe):
            def embed(a):
                pe.wait_ge(patch_in[a.par], a.half * 16 + 16)
                if due(a.no - 2):
                    pe.wait_ge(h2_ready, a.no - 2)
                if due(a.no):
                    pe.wait_ge(lin_ready, a.no)
                for k in range(PK):
                    mm = pe.matmul(tok_ps[0:a.n, 0:D], patch[:, a.par, k * a.n:(k + 1) * a.n], tokw[:, k, :],
                                   start=k == 0, stop=k == PK - 1)
                mm.then_inc(embed_done, 1)

            def turn(n, src):
                pe.transpose(turn_ps[:, 0:n], src[:, 0:P], ident[0:n, 0:n])
                return pe.transpose(turn_ps[0:DB, P:P + n], src[:, P:D], ident[0:n, 0:n])

            def turn_xc(a):
                pe.wait_ge(xc_ready, a.no + 1)
                if due(a.no):
                    pe.wait_ge(xn_ready, a.no)
                if due(a.no - 2):
                    pe.wait_ge(rank_ready, a.no - 2)
                turn(a.n, xc[0:a.n, :]).then_inc(xc_turned, 1)

            def fill(b, f):
                ps = fill_ps[(b.par + f) % 2]
                pe.wait_ge(xn_ready, b.no + 1)
                if due(b.no * FILLS + (f - 1)):
                    pe.wait_ge(fill_read, b.no * FILLS + (f - 1))
                xa, xb = xn_a[:, b.par, 0:b.n], xn_b[0:KB, b.par, 0:b.n]
                if f < UNITS:
                    for c in range(UH):
                        at = (c // 2) * INNER + (2 * f + c % 2) * P
                        o = ps[:, c * GROUP:c * GROUP + b.n]
                        pe.matmul(o, wqkv_a[:, at:at + P], xa, start=True, stop=False)
                        mm = pe.matmul(o, wqkv_b[0:KB, at:at + P], xb, start=False, stop=True)
                else:
                    width = INNER // 2
                    at = 2 * INNER + (f - UNITS) * width
                    pe.matmul(ps[0:b.n, 0:width], xa, wqkv_a[:, at:at + width], start=True, stop=False)
                    mm = pe.matmul(ps[0:b.n, 0:width], xb, wqkv_b[0:KB, at:at + width], start=False, stop=True)
                mm.then_inc(fill_done, 1)

            def scores(g, u):
                no, _ = unit_of(g, u)
                pe.wait_ge(fill_read, g.no * FILLS + (u + 1))
                if due(no):
                    pe.wait_ge(diff_ready, no)
                for e in range(2):
                    pe.matmul(score_ps[0:g.n, e, 0:2 * GROUP], mask_l[:, 0:g.n],
                              mask_r[:, :, :].rearrange("p j s -> p (j s)"), start=True, stop=False,
                              skip_group_check=True)
                for e in range(2):
                    for j in range(2):
                        rows = slice(DH * e, DH * e + DH)
                        mm = pe.matmul(score_ps[0:g.n, e, j * GROUP:j * GROUP + g.n], qk[rows, g.par, u, j, 0:g.n],
                                       qk[rows, g.par, u, 2 + j, 0:g.n], start=False, stop=True, skip_group_check=True)
                mm.then_inc(score_done, 1)

            def turn_prob(g, u):
                no, buf = unit_of(g, u)
                pe.wait_ge(exp_ready, no + 1)
                if due(no):
                    pe.wait_ge(prob_t_ready, no)
                for c in range(UH):
                    mm = pe.transpose(prob_ps[0:g.n, c * GROUP:c * GROUP + g.n], prob[0:g.n, buf, c, 0:g.n],
                                      ident[0:g.n, 0:g.n])
                mm.then_inc(prob_turned, 1)

            def attend(g, u):
                no, buf = unit_of(g, u)
                pe.wait_ge(prob_t_ready, no + 1)
                pe.wait_ge(fill_read, g.no * FILLS + FILLS)
                if due(no):
                    pe.wait_ge(ctx_t_ready, no)
                for c in range(UH):
                    e, j = divmod(c, 2)
                    at = 2 * j + e
                    mm = pe.matmul(ctx_ps[0:g.n, at * (DH + 1):(at + 1) * (DH + 1)], prob_t[0:g.n, buf, c, 0:g.n],
                                   v[0:g.n, g.par, UH * u + at, :], start=True, stop=True)
                mm.then_inc(av_done, 1)

            def turn_ctx(g, u):
                no, buf = unit_of(g, u)
                pe.wait_ge(ctx_ready, no + 1)
                for j in range(2):
                    at = UH * (DH + 1) + j * GROUP
                    mm = pe.transpose(ctx_ps[:, at:at + g.n],
                                      cx[0:g.n, buf, 2 * j:2 * j + 2, :].rearrange("p c t -> p (c t)"),
                                      ident[0:g.n, 0:g.n])
                mm.then_inc(ctx_turned, 1)

            def project(g):
                pe.wait_ge(ctx_t_ready, g.no * UNITS + UNITS)
                pe.wait_ge(lin_ready, min(g.no + 3, GROUPS) if isinstance(g.no, int) else g.no + 3)
                if due(g.no):
                    pe.wait_ge(h2_ready, g.no)
                for k in range(PK):
                    mm = pe.matmul(tok_ps[0:g.n, 0:D], cx_t[:, g.par, k, 0:g.n], wo[:, k, :],
                                   start=k == 0, stop=k == PK - 1)
                mm.then_inc(proj_done, 1)

            def turn_z(d):
                pe.wait_ge(z_ready, d.no + 1)
                pe.wait_ge(xn_ready, min(d.no + 3, GROUPS) if isinstance(d.no, int) else d.no + 3)
                if due(d.no):
                    pe.wait_ge(rank_ready, d.no)
                turn(d.n, z[0:d.n, d.par, :]).then_inc(z_turned, 1)

            def logits(d):
                pe.wait_ge(zt_ready, d.no + 1)
                pe.matmul(turn_ps[0:d.n, 256:256 + EXPERTS], zt_a[:, 0:d.n], wr_a[:, :], start=True, stop=False)
                pe.matmul(turn_ps[0:d.n, 256:256 + EXPERTS], zt_b[0:KB, 0:d.n], wr_b[0:KB, :], start=False,
                          stop=True).then_inc(logits_done, 1)

            def ranks(d):
                pe.wait_ge(chosen_ready, d.no + 1)
                if due(d.no):
                    pe.wait_ge(seen_ready, d.no)
                pe.wait_ge(ldiff_ready, d.no + 1)
                pe.wait_ge(top_i_ready, d.no + 1)
                o = turn_ps[0:d.n, 288:288 + EXPERTS]
                pe.matmul(o, before[0:d.n, 0:d.n], chosen[0:d.n, d.par, :], start=True, stop=False)
                pe.matmul(o, ones[:, 0:d.n], seen[:, d.par, :], start=False, stop=True).then_inc(rank_done, 1)

            def iteration(at, i):
                g, d, b, a = (Group(at + k, i) for k in (0, -1, 1, 2))
                if g.live:
                    scores(g, 0)
                if b.live:
                    fill(b, 0)
                if d.live:
                    turn_z(d)
                if g.live:
                    turn_prob(g, 0)
                    scores(g, 1)
                if a.live:
                    embed(a)
                if d.live:
                    logits(d)
                if g.live:
                    attend(g, 0)
                if b.live:
                    fill(b, 1)
                if g.live:
                    turn_prob(g, 1)
                    scores(g, 2)
                    turn_ctx(g, 0)
                if b.live:
                    fill(b, 2)
                if d.live:
                    ranks(d)
                if g.live:
                    attend(g, 1)
                    turn_prob(g, 2)
                if b.live:
                    fill(b, 3)
                if g.live:
                    turn_ctx(g, 1)
                    attend(g, 2)
                if a.live:
                    turn_xc(a)
                if b.live:
                    fill(b, 4)
                if g.live:
                    turn_ctx(g, 2)
                    project(g)

            pe.wait_ge(tokw_in, 16)
            pe.wait_ge(const, CONSTS + 11)
            pe.wait_ge(qkv_in, 32)
            pe.wait_ge(wo_in, 48)
            pipeline(pe, iteration)

            final = Group(GROUPS - 1)
            pe.wait_ge(seen_ready, GROUPS)
            pe.matmul(tok_ps[0:1, 256:256 + EXPERTS], ones[:, 0:1], seen[:, 1 - final.par, :],
                      start=True, stop=True).then_inc(count_done, 1)

            def turn_tokens(buf, half, n):
                pe.wait_ge(zg_in[buf], half * (16 * WT) + 16 * WT)
                if due(n):
                    pe.wait_ge(xt_ready, n)
                for t in range(WT):
                    pe.transpose(turn_ps[:, t * P:(t + 1) * P], zg[:, buf, t, 0:P], ident[:, :])
                    mm = pe.transpose(turn_ps[0:DB, WINDOW + t * P:WINDOW + (t + 1) * P], zg[:, buf, t, P:D], ident[:, :])
                mm.then_inc(zg_turned, 1)

            pe.sem_inc(hid_done, HID0)
            turn_tokens(0, 0, 0)
            pe.sem_inc(y_done, Y0)
            pe.wait_ge(rounds_ready, 1)
            with pe.Fori(0, pe.value_load(rounds[0:1, 0:1], min_val=1, max_val=ROUNDS)) as r:
                with pe.Fori(0, EXPERTS // 2) as j:
                    for buf in range(2):
                        n = r * EXPERTS + j * 2 + buf
                        half = r * (EXPERTS // 2) + j
                        pe.wait_ge(xt_ready, n + 1)
                        pe.wait_ge(w_in[buf], half * (16 * W_DMAS) + 16 * W_DMAS)
                        for c in range(FK // 2):
                            pe.wait_ge(gelu_ready, n * 3 + (c - 2 + GELU0))
                            for k in (2 * c, 2 * c + 1):
                                o = hid_ps[c][:, (k % 2) * WINDOW:(k % 2 + 1) * WINDOW]
                                cols = slice(k * P, (k + 1) * P)
                                pe.matmul(o, w1_a[:, buf, cols], xt_a[:, buf, :], start=True, stop=False)
                                mm = pe.matmul(o, w1_b[0:KB, buf, cols], xt_b[0:KB, buf, :], start=False, stop=True)
                            mm.then_inc(hid_done, 1)
                        turn_tokens(1 - buf, half + buf, n + 1)
                        pe.wait_ge(y_ready, n - 1 + Y0)
                        for t in range(WT):
                            for k in range(FK):
                                if t == 0 and k % 2 == 0:
                                    pe.wait_ge(gelu_ready, n * 3 + (k // 2 + 1 + GELU0))
                                mm = pe.matmul(score_ps[:, buf, t * D:(t + 1) * D], hid[:, buf, k, t * P:(t + 1) * P],
                                               w2_s[:, buf, k, :], start=k == 0, stop=k == FK - 1)
                        mm.then_inc(y_done, 1)


INPUTS = ["patches", "patches_last", "tok_w", "tok_b", "tok_ln_w", "tok_ln_b", "gamma", "beta", "w_qkv", "w_out",
          "b_out", "w_router", "w1", "b1", "w2", "b2"]


def kernel(x, L0_tok_W, L0_tok_b, L0_tok_ln_w, L0_tok_ln_b, L0_attn_ln_gamma, L0_attn_ln_beta, L0_attn_w_qkv,
           L0_attn_w_out, L0_attn_b_out, L0_ffn_wr, L0_ffn_w1, L0_ffn_b1, L0_ffn_w2, L0_ffn_b2):
    import numpy as np
    import concourse.bacc as bacc
    from concourse.bass_utils import run_bass_kernel_spmd

    def chunked(w):
        w = np.asarray(w)
        return w.T.reshape(-1, P, w.shape[0]).transpose(1, 0, 2).reshape(P, -1)

    G1 = GROUPS - 1
    feats = np.asarray(x).reshape(IMAGES, 3, 6, 16, 6, 16).transpose(1, 3, 5, 0, 2, 4).reshape(PK, P, TOKENS)
    arrays = {
        "patches": feats[:, :, :G1 * GROUP].reshape(PK, P, G1, GROUP).transpose(2, 1, 0, 3).reshape(G1, P, -1),
        "patches_last": feats[:, :, G1 * GROUP:].transpose(1, 0, 2).reshape(P, -1),
        "tok_w": chunked(L0_tok_W),
        "tok_b": L0_tok_b, "tok_ln_w": L0_tok_ln_w, "tok_ln_b": L0_tok_ln_b,
        "gamma": L0_attn_ln_gamma, "beta": L0_attn_ln_beta,
        "w_qkv": np.asarray(L0_attn_w_qkv).T,
        "w_out": chunked(L0_attn_w_out), "b_out": L0_attn_b_out,
        "w_router": np.asarray(L0_ffn_wr).T,
        "w1": np.asarray(L0_ffn_w1).transpose(0, 2, 1), "b1": L0_ffn_b1,
        "w2": np.asarray(L0_ffn_w2).reshape(EXPERTS, D, FK, P).transpose(0, 3, 2, 1).reshape(EXPERTS, P, -1),
        "b2": L0_ffn_b2,
    }
    nc = bacc.Bacc("TRN2", target_bir_lowering=False, num_devices=1)
    given, args = {}, []
    for name in INPUTS:
        a = np.ascontiguousarray(arrays[name])
        given[f"in_{name}"] = a
        args.append(nc.dram_tensor(f"in_{name}", a.shape, mybir.dt.from_np(a.dtype), kind="ExternalInput").ap())
    args.append(nc.dram_tensor("out_0", (TOKENS, D), F32, kind="ExternalOutput").ap())
    vit_block(nc, *args)
    r = run_bass_kernel_spmd(nc, [given], core_ids=[0])
    return r.results[0]["out_0"].reshape(IMAGES, IMAGE, D)
```

```python
from contextlib import ExitStack

import concourse.bass as bass
from concourse import mybir

F32 = mybir.dt.float32
BF16 = mybir.dt.bfloat16
F16 = mybir.dt.float16
I32 = mybir.dt.int32
U32 = mybir.dt.uint32
ALU = mybir.AluOpType
ACT = mybir.ActivationFunctionType
AX = mybir.AxisListType

P = 128
IMAGES = 32
IMAGE = 36
TOKENS = IMAGES * IMAGE
PER_GROUP = 3
GROUP = PER_GROUP * IMAGE
GROUPS = -(-TOKENS // GROUP)
LAST = TOKENS - (GROUPS - 1) * GROUP
D = 192
DB = D - P
KB = DB + 1
PATCH = 768
PK = PATCH // P
HEADS = 12
DH = 64
INNER = HEADS * DH
UNITS = 3
UH = HEADS // UNITS
EXPERTS = 16
F = 768
FK = F // P
TOPK = 2
EPS = 1e-5
MASKED = -1e30

WINDOW = 256
WT = WINDOW // P
ROUNDS = -(-TOKENS // WINDOW)
QS = ROUNDS * WT
ROW = EXPERTS * QS
SLOTS = P * ROW
PAIRS = TOPK * TOKENS

HIGH = slice(0, D)
LOWS = ((slice(D, 2 * P), slice(P, D)), (slice(2 * P, 3 * P), slice(0, P)))

QKV_PIECES = [(0, slice(0, 2 * INNER)), (1, slice(0, 2 * INNER)),
              (0, slice(2 * INNER, 3 * INNER)), (1, slice(2 * INNER, 3 * INNER))]

FILLS = 5
CHUNKS = [(0, 3), (3, 7), (7, GROUPS - 1), (GROUPS - 1, GROUPS)]
LOOPED = 2
FIRST_LOOPED = 3


class Group:

    def __init__(self, at, i=None):
        self.no = at if i is None else i * 2 + at
        self.par = at % 2
        self.half = at // 2 if i is None else i + at // 2
        self.live = i is not None or 0 <= at < GROUPS
        self.n = LAST if i is None and at == GROUPS - 1 else GROUP


def due(count):
    return not isinstance(count, int) or count > 0


def held(eng, count):
    return count if isinstance(count, int) else eng.to_reg(count)


def pipeline(eng, iteration):
    for at in range(-2, FIRST_LOOPED):
        iteration(at, None)
    with eng.Fori(0, LOOPED) as i:
        iteration(FIRST_LOOPED, i)
        iteration(FIRST_LOOPED + 1, i)
    for at in range(FIRST_LOOPED + 2 * LOOPED, GROUPS + 1):
        iteration(at, None)


def vit_block(nc, patches, patches_last, tok_w, tok_b, tok_ln_w, tok_ln_b, gamma, beta, w_qkv, w_out, b_out,
              w_router, w1, w2, b2, out):
    z_rows = nc.dram_tensor("z_rows", [TOKENS, 2 * D], F16, kind="Internal").ap()
    slot_table = nc.dram_tensor("slot_table", [SLOTS, 1], I32, kind="Internal").ap()
    y_rows = nc.dram_tensor("y_rows", [PAIRS + SLOTS, D], F32, kind="Internal").ap()

    with ExitStack() as ctx:
        def sb(name, shape, dt=F32):
            return ctx.enter_context(nc.sbuf_tensor(name, shape, dt))

        def bank(name, *dims):
            return ctx.enter_context(nc.psum_tensor(name, [P, *(dims or (512,))], F32))

        def sem(name):
            return ctx.enter_context(nc.semaphore(name))

        tokw = sb("tokw", [P, PK, D])
        stage = sb("stage", [P, 2, 3 * INNER])
        wqkv = sb("wqkv", [P, 2, 2, 3 * INNER], F16)
        wo = sb("wo", [P, PK, D])
        wr_a = sb("wr_a", [P, EXPERTS])
        wr_b = sb("wr_b", [P, EXPERTS])
        tokb = sb("tokb", [P, D])
        lnw = sb("lnw", [P, D])
        lnb = sb("lnb", [P, D])
        bo = sb("bo", [P, D])
        gam = sb("gam", [P, D])
        bet = sb("bet", [P, D])
        b2all = sb("b2all", [P, EXPERTS, D])
        ident = sb("ident", [P, P])
        ident16 = sb("ident16", [P, P], F16)
        before = sb("before", [P, P], BF16)
        ones = sb("ones", [P, P], BF16)
        mask_l = sb("mask_l", [P, GROUP], BF16)
        mask_r = sb("mask_r", [P, 2, GROUP], BF16)
        minus_half = sb("minus_half", [P, 1])
        experts = sb("experts", [P, EXPERTS])
        pairs = sb("pairs", [P, GROUPS, TOPK], I32)
        pads = sb("pads", [P, ROW], I32)

        patch = sb("patch", [P, 2, PK * GROUP])
        lin = sb("lin", [P, D])
        lnc = sb("lnc", [P, D])
        h = sb("h", [P, 2, D])
        xc = sb("xc", [P, D])
        xf = sb("xf", [P, D])
        xs = sb("xs", [P, 2 * D], F16)
        st1, st2, st4 = (sb(f"st{k}", [P, 6]) for k in (1, 2, 4))
        mv1, mv2, mv4 = (sb(f"mv{k}", [P, 2]) for k in (1, 2, 4))
        ve1, ve2, ve4 = (sb(f"ve{k}", [P, 1]) for k in (1, 2, 4))
        rs1, rs2, rs4 = (sb(f"rs{k}", [P, 1]) for k in (1, 2, 4))
        hb_all = sb("hb_all", [P, GROUPS, D])
        xn = sb("xn", [P, 2, 3, GROUP], F16)
        qk = sb("qk", [P, 2, UNITS, UH, GROUP])
        v = sb("v", [P, 2, HEADS, DH + 1])
        nmax = sb("nmax", [P, 2, UH])
        prob = sb("prob", [P, 2, UH, GROUP])
        prob_t = sb("prob_t", [P, 2, UH, GROUP])
        rsum = sb("rsum", [P, UH])
        cx = sb("cx", [P, 2, UH, DH])
        cx_t = sb("cx_t", [P, 2, PK, GROUP])
        h2 = sb("h2", [P, 2, D])
        z = sb("z", [P, 2, D])
        zs = sb("zs", [P, 2, 2 * D], F16)
        zt_a = sb("zt_a", [P, GROUP])
        zt_b = sb("zt_b", [P, GROUP])
        base_all = sb("base_all", [P, GROUPS, D])
        gates_all = sb("gates_all", [P, GROUPS, TOPK])
        top = sb("top", [P, 8])
        top_i = sb("top_i", [P, 8], U32)
        top_e = sb("top_e", [P, TOPK])
        ldiff = sb("ldiff", [P, EXPERTS + TOPK])
        lexp = sb("lexp", [P, EXPERTS + TOPK])
        lsum = sb("lsum", [P, 1])
        lrec = sb("lrec", [P, 1])
        onehot = sb("onehot", [P, TOPK, EXPERTS])
        chosen = sb("chosen", [P, 2, EXPERTS], BF16)
        seen = sb("seen", [P, 2, EXPERTS], BF16)
        rank_e = sb("rank_e", [P, TOPK, EXPERTS])
        rank = sb("rank", [P, TOPK])
        rank_i = sb("rank_i", [P, TOPK], I32)
        block_i = sb("block_i", [P, TOPK], I32)
        rank_w = sb("rank_w", [P, TOPK])
        slot_f = sb("slot_f", [P, TOPK])
        slot = sb("slot", [P, 2, TOPK], I32)
        pair = sb("pair", [P, 2, TOPK], I32)
        most = sb("most", [1, 1])
        most_i = sb("most_i", [1, 1], I32)
        rounds = sb("rounds", [1, 1], I32)
        table = sb("table", [P, ROW], I32)
        table_h = sb("table_h", [P, ROW], I32)
        table_z = sb("table_z", [P, ROW], I32)
        w1_s = sb("w1_s", [P, 2, 2, 2, F], F16)
        w2_s = sb("w2_s", [P, 2, FK * D + FK])
        from_row = sb("from_row", [P, 2, WT], I32)
        to_row = sb("to_row", [P, 2, WT], I32)
        zg = sb("zg", [P, 2, WT, 2 * D], F16)
        xt = sb("xt", [P, 2, 3, WINDOW], F16)
        hid = sb("hid", [P, 2, FK, WINDOW])
        y = sb("y", [P, 2, WT, D])
        y_back = sb("y_back", [P, GROUPS, TOPK * D])
        part = sb("part", [P, GROUPS, D])
        second = sb("second", [P, GROUPS, D])

        tok_ps = bank("tok_ps")
        turn_ps = bank("turn_ps")
        fill_ps = [bank("fill0_ps"), bank("fill1_ps")]
        score_ps = bank("score_ps", 2, 512)
        prob_ps = bank("prob_ps")
        ctx_ps = bank("ctx_ps")
        turn16_ps = turn_ps[:, :].bitcast(F16)
        w1_stage = stage[:, :, 0:2 * F]
        hid_ps = [fill_ps[0], fill_ps[1], prob_ps]

        tokw_in, rows_in, wo_in = sem("tokw_in"), sem("rows_in"), sem("wo_in")
        qkv_in = [sem(f"qkv_in{piece}") for piece in range(4)]
        b2_in = sem("b2_in")
        patch_in = [sem("patch_in0"), sem("patch_in1")]
        begun = sem("begun")
        const = sem("const")
        pads_made, pads_out = sem("pads_made"), sem("pads_out")
        zeroed = sem("zeroed")
        embed_done, xc_turned, fill_done = sem("embed_done"), sem("xc_turned"), sem("fill_done")
        score_done, prob_turned, av_done = sem("score_done"), sem("prob_turned"), sem("av_done")
        ctx_turned, proj_done, z_turned = sem("ctx_turned"), sem("proj_done"), sem("z_turned")
        logits_done, rank_done, count_done = sem("logits_done"), sem("rank_done"), sem("count_done")
        hid_done, zg_turned, y_done = sem("hid_done"), sem("zg_turned"), sem("y_done")
        qkv_high, w1_high = sem("qkv_high"), sem("w1_high")
        xn_ready, fill_read, exp_ready = sem("xn_ready"), sem("fill_read"), sem("exp_ready")
        prob_t_ready, ctx_t_ready, zt_ready = sem("prob_t_ready"), sem("ctx_t_ready"), sem("zt_ready")
        lexp_ready, gelu_ready = sem("lexp_ready"), sem("gelu_ready")
        qkv_low, w1_low = sem("qkv_low"), sem("w1_low")
        xf_ready, xs_high, xs_ready = sem("xf_ready"), sem("xs_high"), sem("xs_ready")
        lin_ready, st1_ready, mv1_ready, lnc_ready, h_ready = (
            sem(s) for s in ("lin_ready", "st1_ready", "mv1_ready", "lnc_ready", "h_ready"))
        st2_ready, mv2_ready, xc_ready = sem("st2_ready"), sem("mv2_ready"), sem("xc_ready")
        max_ready, diff_ready, rsum_ready, ctx_ready = (
            sem(s) for s in ("max_ready", "diff_ready", "rsum_ready", "ctx_ready"))
        h2_ready, st4_ready, mv4_ready, z_ready = (
            sem(s) for s in ("h2_ready", "st4_ready", "mv4_ready", "z_ready"))
        top_ready, top_i_ready, top_e_ready, ldiff_ready = (
            sem(s) for s in ("top_ready", "top_i_ready", "top_e_ready", "ldiff_ready"))
        lsum_ready, lrec_ready, gates_ready = sem("lsum_ready"), sem("lrec_ready"), sem("gates_ready")
        onehot_ready, chosen_ready, seen_ready = sem("onehot_ready"), sem("chosen_ready"), sem("seen_ready")
        rank_ready, rank_i_ready, block_ready, slot_f_ready, slot_ready = (
            sem(s) for s in ("rank_ready", "rank_i_ready", "block_ready", "slot_f_ready", "slot_ready"))
        most_ready, most_i_ready, rounds_ready = sem("most_ready"), sem("most_i_ready"), sem("rounds_ready")
        halved, rows_ready = sem("halved"), sem("rows_ready")
        xt_ready, y_ready = sem("xt_ready"), sem("y_ready")
        part_ready, result_ready = sem("part_ready"), sem("result_ready")
        second_ready = sem("second_ready")
        ve1_ready, rs1_ready, ve2_ready, rs2_ready, ve4_ready, rs4_ready = (
            sem(s) for s in ("ve1_ready", "rs1_ready", "ve2_ready", "rs2_ready", "ve4_ready", "rs4_ready"))
        hb_ready, base_ready, pair_ready = sem("hb_ready"), sem("base_ready"), sem("pair_ready")
        zs_high, zs_ready, v_low = sem("zs_high"), sem("zs_ready"), sem("v_low")
        from_ready, to_ready = sem("from_ready"), sem("to_ready")
        z_out = [sem("z_out0"), sem("z_out1")]
        scattered = [sem("scattered0"), sem("scattered1")]
        table_in = sem("table_in")
        w1_in = [sem("w1_in0"), sem("w1_in1")]
        w2_in = [sem("w2_in0"), sem("w2_in1")]
        zg_in = [sem("zg_in0"), sem("zg_in1")]
        y_in = [sem(f"y_in{k}") for k in range(len(CHUNKS))]
        all_out = sem("all_out")

        CONSTS = 7
        Y0 = 2
        GELU0 = 3
        HID0 = 1
        TO0 = 1
        SLOTS0 = [16 * TOPK * ((GROUPS + 1 - buf) // 2) for buf in range(2)]

        def unit_of(g, u):
            return UNITS * g.no + u, (g.par + u) % 2

        def scores_view(n):
            return score_ps[0:n, :, 0:2 * GROUP].rearrange("p e (j s) -> p e j s", j=2)[:, :, :, 0:n]

        def prob_view(tile, buf, n):
            return tile[0:n, buf, :, 0:n].rearrange("p (e j) s -> p e j s", e=2)

        block = ctx.enter_context(nc.Block())

        @block.sync
        def _(sp):
            def load_patches(a):
                count = held(sp, a.no - 1)
                sp.wait_ge(begun, 1)
                if due(count):
                    sp.wait_ge(embed_done, count)
                dst = patch[:, a.par, 0:PK * a.n]
                src = patches_last if a.n == LAST else patches[bass.ds(a.no, 1)].rearrange("a p n -> (a p) n")
                sp.dma_start(dst, src).then_inc(patch_in[a.par], 16)

            sp.dma_start(tokw[:, :, :], tok_w.rearrange("p (k n) -> p k n", k=PK)).then_inc(tokw_in, 16)
            load_patches(Group(0))
            load_patches(Group(1))
            for tile, row in ((tokb, tok_b), (lnw, tok_ln_w), (lnb, tok_ln_b), (gam, gamma), (bet, beta),
                              (bo, b_out)):
                sp.dma_start(tile[:, :], row.rearrange("(a n) -> a n", a=1).to_broadcast([P, D])).then_inc(rows_in, 16)
            for piece, (c, cols) in enumerate(QKV_PIECES):
                sp.dma_start(stage[:, c, cols], w_qkv.rearrange("p (c n) -> p c n", c=2)[:, c, cols]
                             ).then_inc(qkv_in[piece], 16)
            sp.dma_start(wo[:, :, :], w_out.rearrange("p (k n) -> p k n", k=PK)).then_inc(wo_in, 16)
            sp.dma_start(wr_a[:, :], w_router[0:P, :]).then_inc(wo_in, 16)
            sp.dma_start(wr_b[0:DB, :], w_router[P:D, :]).then_inc(wo_in, 16)
            sp.wait_ge(pads_made, 1)
            sp.dma_start(slot_table.rearrange("(p s) a -> p (s a)", p=P), pads[:, :]).then_inc(pads_out, 16)
            sp.dma_start(b2all[:, :, :], b2.rearrange("e n -> (e n)").rearrange("(a n) -> a n", a=1)
                         .to_broadcast([P, EXPERTS * D]).rearrange("p (e n) -> p e n", e=EXPERTS)).then_inc(b2_in, 16)

            def load_expert(buf, e, n):
                one = bass.ds(e, 1)
                if not isinstance(n, int):
                    sp.wait_ge(w1_low, n - 1)
                sp.dma_start(w1_stage[:, buf, :], w1[one].rearrange("a p n -> (a p) n")).then_inc(w1_in[buf], 16)
                if not isinstance(n, int):
                    sp.wait_ge(y_done, n - 1 + Y0)
                sp.dma_start(w2_s[:, buf, :], w2[one].rearrange("a p n -> (a p) n")).then_inc(w2_in[buf], 16)

            def iteration(at, i):
                d, a = Group(at - 1, i), Group(at + 2, i)
                if a.live and at >= 0:
                    load_patches(a)
                if at == FIRST_LOOPED + 2 * LOOPED:
                    sp.wait_ge(qkv_low, 2)
                    sp.wait_ge(v_low, 2)
                    load_expert(0, 0, 0)
                    load_expert(1, 1, 1)
                if d.live:
                    sp.wait_ge(zs_ready, d.no + 1)
                    sp.dma_start(z_rows[bass.ds(d.no * GROUP, d.n), :],
                                 zs[0:d.n, d.par, :]).then_inc(z_out[d.par], 16)

            pipeline(sp, iteration)

            for buf in range(2):
                sp.wait_ge(scattered[buf], SLOTS0[buf])
            sp.dma_start(table[:, :], slot_table.rearrange("(p s) a -> p (s a)", p=P)).then_inc(table_in, 16)
            sp.wait_ge(rounds_ready, 1)
            with sp.Fori(0, sp.value_load(rounds[0:1, 0:1], min_val=1, max_val=ROUNDS)) as r:
                with sp.Fori(0, EXPERTS // 2 - 1) as j:
                    for buf in range(2):
                        load_expert(buf, j * 2 + (2 + buf), r * EXPERTS + j * 2 + (2 + buf))
                for buf in range(2):
                    load_expert(buf, buf, r * EXPERTS + (EXPERTS + buf))
            steps = sp.value_load(rounds[0:1, 0:1], min_val=1, max_val=ROUNDS) * (EXPERTS // 2)
            for buf in range(2):
                count, count_y = held(sp, steps * 16 + 16), held(sp, steps * (16 * WT) + SLOTS0[buf])
                sp.wait_ge(begun, 1)
                sp.wait_ge(w1_in[buf], count)
                sp.wait_ge(w2_in[buf], count)
                sp.wait_ge(scattered[buf], count_y)
            rows = y_rows[0:PAIRS, :].rearrange("(t k) n -> t (k n)", k=TOPK)
            for k, (first, last) in enumerate(CHUNKS):
                n = Group(first).n
                sp.dma_start(y_back[0:n, first:last, :],
                             rows[first * GROUP:first * GROUP + n * (last - first), :]
                             .rearrange("(g t) n -> t g n", t=n)).then_inc(y_in[k], 16)
            for k, (first, last) in enumerate(CHUNKS):
                n = Group(first).n
                sp.wait_ge(result_ready, k + 1)
                sp.dma_start(out[first * GROUP:first * GROUP + n * (last - first), :]
                             .rearrange("(g t) n -> t g n", t=n), part[0:n, first:last, :]).then_inc(all_out, 16)
            sp.wait_ge(all_out, 16 * len(CHUNKS))

        @block.gpsimd
        def _(pool):
            pool.memset(ident[:, :], 0.0).then_inc(begun, 1)
            pool.memset(ident16[:, :], 0.0).then_inc(zeroed, 1)
            pool.memset(before[:, :], 1.0).then_inc(zeroed, 1)
            pool.memset(mask_l[:, :], 1.0).then_inc(zeroed, 1)
            pool.memset(mask_r[:, :, :], 0.0).then_inc(zeroed, 1)
            pool.memset(ones[:, :], 1.0).then_inc(const, 1)
            pool.memset(minus_half[:, :], -0.5).then_inc(const, 1)
            pool.wait_ge(begun, 1)
            pool.wait_ge(zeroed, 4)
            for tile in (ident, ident16):
                pool.affine_select(out=tile[:, :], in_=tile[:, :], compare_op=ALU.not_equal, fill=1.0,
                                   base=0, pattern=[[-1, P]], channel_multiplier=1).then_inc(const, 1)
            pool.affine_select(out=before[:, :], in_=before[:, :], compare_op=ALU.is_gt, fill=0.0,
                               base=0, pattern=[[1, P]], channel_multiplier=-1).then_inc(const, 1)
            pool.affine_select(out=mask_l[:, :], in_=mask_l[:, :], compare_op=ALU.is_ge, fill=0.0,
                               base=0, pattern=[[1, GROUP]], channel_multiplier=-IMAGE).then_inc(zeroed, 1)
            pool.affine_select(out=mask_r[:, :, :], in_=mask_r[:, :, :], compare_op=ALU.is_ge, fill=MASKED,
                               base=0, pattern=[[0, 2], [1, GROUP]], channel_multiplier=-IMAGE).then_inc(zeroed, 1)
            pool.wait_ge(zeroed, 6)
            pool.affine_select(out=mask_l[:, :], in_=mask_l[:, :], compare_op=ALU.is_ge, fill=0.0,
                               base=IMAGE - 1, pattern=[[-1, GROUP]], channel_multiplier=IMAGE).then_inc(const, 1)
            pool.affine_select(out=mask_r[:, :, :], in_=mask_r[:, :, :], compare_op=ALU.is_ge, fill=MASKED,
                               base=IMAGE - 1, pattern=[[0, 2], [-1, GROUP]],
                               channel_multiplier=IMAGE).then_inc(const, 1)
            pool.iota(pads[:, :], pattern=[[1, ROW]], base=PAIRS, channel_multiplier=ROW).then_inc(pads_made, 1)
            pool.iota(pairs[:, :, :], pattern=[[TOPK * GROUP, GROUPS], [1, TOPK]], base=0,
                      channel_multiplier=TOPK).then_inc(pads_made, 1)
            pool.wait_ge(pads_made, 2)

            def rsqrt(n, mv, scale, shift, ve, ve_ready, rs, rs_ready, no):
                pool.tensor_scalar(ve[0:n, :], mv[0:n, 1:2], scale, shift, ALU.mult, ALU.add).then_inc(ve_ready, 1)
                pool.wait_ge(ve_ready, no + 1)
                pool.tensor_tensor(rs[0:n, :], ve[0:n, :], minus_half[0:n, :], ALU.pow).then_inc(rs_ready, 1)

            def iteration(at, i):
                d, a = Group(at - 1, i), Group(at + 2, i)
                if at == -1:
                    for piece, (c, cols) in enumerate(QKV_PIECES[2:], 2):
                        pool.wait_ge(qkv_high, piece + 1)
                        pool.tensor_tensor(wqkv[:, 1, c, cols], stage[:, c, cols], wqkv[:, 0, c, cols],
                                           ALU.subtract).then_inc(v_low, 1)
                if d.live:
                    count, count_free = held(pool, d.no + 1), held(pool, d.no)
                    pool.wait_ge(begun, 1)
                    pool.wait_ge(mv4_ready, count)
                    if due(count_free):
                        pool.wait_ge(z_ready, count_free)
                    rsqrt(d.n, mv4, 1.0, EPS, ve4, ve4_ready, rs4, rs4_ready, d.no)
                if d.live:
                    count, count_free = held(pool, d.no + 1), held(pool, d.half * 16)
                    pool.wait_ge(begun, 1)
                    pool.wait_ge(z_ready, count)
                    if due(count_free):
                        pool.wait_ge(z_out[d.par], count_free)
                    pool.tensor_copy(zs[0:d.n, d.par, HIGH], z[0:d.n, d.par, :]).then_inc(zs_high, 1)
                    pool.wait_ge(zs_high, d.no + 1)
                    for low, cols in LOWS:
                        op = pool.tensor_tensor(zs[0:d.n, d.par, low], z[0:d.n, d.par, cols], zs[0:d.n, d.par, cols],
                                                ALU.subtract)
                    op.then_inc(zs_ready, 1)
                    pool.tensor_tensor(base_all[0:d.n, bass.ds(d.no, 1), :].rearrange("p a n -> p (a n)"),
                                       h2[0:d.n, d.par, :], z[0:d.n, d.par, :], ALU.add).then_inc(base_ready, 1)
                if a.live:
                    count, count_free = held(pool, a.no + 1), held(pool, a.no)
                    pool.wait_ge(begun, 1)
                    pool.wait_ge(mv1_ready, count)
                    if due(count_free):
                        pool.wait_ge(h_ready, count_free)
                    rsqrt(a.n, mv1, 1.0, EPS, ve1, ve1_ready, rs1, rs1_ready, a.no)
                    count, count_free = held(pool, a.no + 1), held(pool, a.no)
                    pool.wait_ge(begun, 1)
                    pool.wait_ge(mv2_ready, count)
                    if due(count_free):
                        pool.wait_ge(xf_ready, count_free)
                    rsqrt(a.n, mv2, 1.0 + EPS, EPS * EPS, ve2, ve2_ready, rs2, rs2_ready, a.no)
                    if at == -2:
                        pool.wait_ge(rows_in, 16 * 6)
                    pool.tensor_tensor(hb_all[0:a.n, bass.ds(a.no, 1), :].rearrange("p a n -> p (a n)"),
                                       h[0:a.n, a.par, :], bo[0:a.n, :], ALU.add).then_inc(hb_ready, 1)
                if d.live:
                    if due(d.half * (16 * TOPK)):
                        pool.wait_ge(scattered[d.par], d.half * (16 * TOPK))
                    pool.tensor_copy(pair[0:d.n, d.par, :],
                                     pairs[0:d.n, bass.ds(d.no, 1), :].rearrange("p a n -> p (a n)")
                                     ).then_inc(pair_ready, 1)
                    count, count_free = held(pool, d.no + 1), held(pool, d.no + 1)
                    pool.wait_ge(begun, 1)
                    pool.wait_ge(pair_ready, count)
                    pool.wait_ge(slot_ready, count_free)
                    if at == 1:
                        pool.wait_ge(pads_out, 16)
                    for k in range(TOPK):
                        pool.indirect_dma_start(
                            slot_table, bass.IndirectOffsetOnAxis(ap=slot[0:d.n, d.par, k:k + 1], axis=0),
                            pair[0:d.n, d.par, k:k + 1], None).then_inc(scattered[d.par], 16)

            pipeline(pool, iteration)

            def gather(buf, col, n):
                pool.tensor_copy(from_row[:, buf, :], table_z[:, bass.ds(col, WT)]).then_inc(from_ready, 1)
                count = held(pool, n + 1)
                pool.wait_ge(begun, 1)
                pool.wait_ge(from_ready, count)
                for t in range(WT):
                    pool.indirect_dma_start(
                        zg[:, buf, t, :], None, z_rows,
                        bass.IndirectOffsetOnAxis(ap=from_row[:, buf, t:t + 1], axis=0)).then_inc(zg_in[buf], 16)

            pool.sem_inc(to_ready, TO0)
            pool.wait_ge(rows_ready, 1)
            for buf in range(2):
                pool.wait_ge(z_out[buf], 16 * ((GROUPS + 1 - buf) // 2))
            gather(0, 0, 0)
            gather(1, QS, 1)
            pool.wait_ge(rounds_ready, 1)
            with pool.Fori(0, pool.value_load(rounds[0:1, 0:1], min_val=1, max_val=ROUNDS)) as r:
                def pair_of_experts(j, last):
                    half = r * (EXPERTS // 2) + j
                    for buf in range(2):
                        n = r * EXPERTS + j * 2 + buf
                        pool.wait_ge(zg_in[buf], half * (16 * WT) + 16 * WT)
                        pool.wait_ge(zg_turned, n + 1)
                        col = r * WT + (WT + buf * QS) if last else j * (2 * QS) + ((2 + buf) * QS) + r * WT
                        gather(buf, col, n + 2)
                        pool.wait_ge(scattered[1 - buf], (half + buf) * (16 * WT) + SLOTS0[1 - buf])
                        pool.tensor_copy(to_row[:, buf, :], table[:, bass.ds(j * (2 * QS) + buf * QS + r * WT, WT)]
                                         ).then_inc(to_ready, 1)
                        count, count_y = held(pool, n + (1 + TO0)), held(pool, n + (1 + Y0))
                        pool.wait_ge(begun, 1)
                        pool.wait_ge(to_ready, count)
                        pool.wait_ge(y_ready, count_y)
                        for t in range(WT):
                            pool.indirect_dma_start(
                                y_rows, bass.IndirectOffsetOnAxis(ap=to_row[:, buf, t:t + 1], axis=0),
                                y[:, buf, t, :], None).then_inc(scattered[buf], 16)

                with pool.Fori(0, EXPERTS // 2 - 1) as j:
                    pair_of_experts(j, False)
                pair_of_experts(EXPERTS // 2 - 1, True)
            halves = pool.value_load(rounds[0:1, 0:1], min_val=1, max_val=ROUNDS) * (EXPERTS // 2)
            for buf in range(2):
                pool.wait_ge(zg_in[buf], halves * (16 * WT) + 16 * WT)

        @block.scalar
        def _(act):
            def turn_xn(a):
                act.wait_ge(xc_turned, a.no + 1)
                if due(a.no * FILLS - FILLS):
                    act.wait_ge(fill_done, a.no * FILLS - FILLS)
                act.activation(xn[:, a.par, :, 0:a.n],
                               turn16_ps[:, 0:3 * GROUP].rearrange("p (c t) -> p c t", c=3)[:, :, 0:a.n],
                               ACT.Copy).then_inc(xn_ready, 1)

            def read_fill(b, f):
                ps = fill_ps[(b.par + f) % 2]
                act.wait_ge(fill_done, b.no * FILLS + (f + 1))
                if f < UNITS:
                    if due(b.no * UNITS + (f + 1 - 2 * UNITS)):
                        act.wait_ge(score_done, b.no * UNITS + (f + 1 - 2 * UNITS))
                    act.activation(qk[:, b.par, f, :, 0:b.n],
                                   ps[:, 0:UH * GROUP].rearrange("p (c t) -> p c t", c=UH)[:, :, 0:b.n],
                                   ACT.Copy).then_inc(fill_read, 1)
                else:
                    half = HEADS // 2
                    if due(b.no * UNITS + (UNITS - 2 * UNITS)):
                        act.wait_ge(av_done, b.no * UNITS + (UNITS - 2 * UNITS))
                    act.activation(v[0:b.n, b.par, (f - UNITS) * half:(f - UNITS + 1) * half, 0:DH],
                                   ps[0:b.n, 0:half * DH].rearrange("p (c t) -> p c t", c=half),
                                   ACT.Copy).then_inc(fill_read, 1)

            def exp(g, u):
                no, buf = unit_of(g, u)
                act.wait_ge(diff_ready, no + 1)
                act.activation(prob[0:g.n, buf, :, 0:g.n], prob[0:g.n, buf, :, 0:g.n], ACT.Exp,
                               scale=DH ** -0.5).then_inc(exp_ready, 1)

            def turn_prob(g, u):
                no, buf = unit_of(g, u)
                act.wait_ge(prob_turned, no + 1)
                if due(no - 1):
                    act.wait_ge(av_done, no - 1)
                act.activation(prob_t[0:g.n, buf, :, 0:g.n],
                               prob_ps[0:g.n, 0:UH * GROUP].rearrange("p (c t) -> p c t", c=UH)[:, :, 0:g.n],
                               ACT.Copy).then_inc(prob_t_ready, 1)

            def turn_ctx(g, u):
                no, _ = unit_of(g, u)
                act.wait_ge(ctx_turned, no + 1)
                if due(g.no - 1):
                    act.wait_ge(proj_done, g.no - 1)
                act.activation(cx_t[:, g.par, 2 * u:2 * u + 2, 0:g.n],
                               ctx_ps[:, UH * (DH + 1):UH * (DH + 1) + 2 * GROUP]
                               .rearrange("p (c t) -> p c t", c=2)[:, :, 0:g.n], ACT.Copy).then_inc(ctx_t_ready, 1)

            def turn_z(d):
                act.wait_ge(z_turned, d.no + 1)
                if due(d.no):
                    act.wait_ge(logits_done, d.no)
                act.activation(zt_a[:, 0:d.n], turn_ps[:, 0:d.n], ACT.Copy)
                act.activation(zt_b[0:DB, 0:d.n], turn_ps[0:DB, P:P + d.n], ACT.Copy).then_inc(zt_ready, 1)

            def high(buf, c, half):
                act.wait_ge(w1_in[buf], half * 16 + 16)
                return act.activation(w1_s[:, buf, 0, c, :], w1_stage[:, buf, c * F:(c + 1) * F], ACT.Copy)

            def router_exp(d):
                act.wait_ge(ldiff_ready, d.no + 1)
                if due(d.no):
                    act.wait_ge(gates_ready, d.no)
                act.activation(lexp[0:d.n, :], ldiff[0:d.n, :], ACT.Exp).then_inc(lexp_ready, 1)

            def iteration(at, i):
                g, d, b, a = (Group(at + k, i) for k in (0, -1, 1, 2))
                if d.live:
                    turn_ctx(d, 2)
                if g.live:
                    turn_prob(g, 0)
                    exp(g, 1)
                    turn_ctx(g, 0)
                    turn_prob(g, 1)
                    exp(g, 2)
                if b.live:
                    read_fill(b, 0)
                if d.live:
                    turn_z(d)
                if b.live:
                    read_fill(b, 1)
                if g.live:
                    turn_ctx(g, 1)
                    turn_prob(g, 2)
                if b.live:
                    read_fill(b, 2)
                    exp(b, 0)
                if d.live:
                    router_exp(d)
                if b.live:
                    read_fill(b, 3)
                if b.live:
                    read_fill(b, 4)
                if a.live:
                    turn_xn(a)
                if at == GROUPS - 1:
                    for c in range(2):
                        high(0, c, 0).then_inc(w1_high, 1)

            for piece, (c, cols) in enumerate(QKV_PIECES):
                act.wait_ge(qkv_in[piece], 16)
                act.activation(wqkv[:, 0, c, cols], stage[:, c, cols], ACT.Copy).then_inc(qkv_high, 1)
            pipeline(act, iteration)

            act.sem_inc(gelu_ready, GELU0)
            act.wait_ge(rounds_ready, 1)
            with act.Fori(0, act.value_load(rounds[0:1, 0:1], min_val=1, max_val=ROUNDS)) as r:
                with act.Fori(0, EXPERTS // 2) as j:
                    for buf in range(2):
                        n = r * EXPERTS + j * 2 + buf
                        half = r * (EXPERTS // 2) + j
                        act.wait_ge(y_done, n - 1 + Y0)
                        act.wait_ge(w2_in[buf], half * 16 + 16)
                        for c in range(FK // 2):
                            if c < 2:
                                if c == 0:
                                    act.wait_ge(hid_done, n * 3 + HID0)
                                high(1 - buf, c, half + buf).then_inc(w1_high, 1)
                            act.wait_ge(hid_done, n * 3 + (c + 1 + HID0))
                            for k in (2 * c, 2 * c + 1):
                                op = act.activation(hid[:, buf, k, :],
                                                    hid_ps[c][:, (k % 2) * WINDOW:(k % 2 + 1) * WINDOW], ACT.Gelu,
                                                    bias=w2_s[:, buf, FK * D + k:FK * D + k + 1])
                            op.then_inc(gelu_ready, 1)

            act.wait_ge(gates_ready, GROUPS)
            for k, (first, last) in enumerate(CHUNKS):
                act.wait_ge(y_in[k], 16)
                for at in range(first, last):
                    n = Group(at).n
                    act.activation(second[0:n, at, :], y_back[0:n, at, D:2 * D], ACT.Copy,
                                   scale=gates_all[0:n, at, 1:2]).then_inc(second_ready, 1)

        @block.vector
        def _(dve):
            dve.memset(v[:, :, :, DH:DH + 1], 1.0).then_inc(const, 1)
            dve.memset(zt_b[DB:KB, :], 0.0).then_inc(const, 1)
            dve.memset(wr_b[DB:KB, :], 0.0).then_inc(const, 1)
            dve.memset(seen[:, :, :], 0.0).then_inc(const, 1)
            dve.memset(experts[:, :], 0.0).then_inc(const, 1)

            def embed_stats(a):
                dve.wait_ge(embed_done, a.no + 1)
                dve.tensor_tensor(lin[0:a.n, :], tok_ps[0:a.n, 0:D], tokb[0:a.n, :], ALU.add).then_inc(lin_ready, 1)
                dve.wait_ge(lin_ready, a.no + 1)
                dve.bn_stats(st1[0:a.n, :], lin[0:a.n, :]).then_inc(st1_ready, 1)
                count = held(dve, a.no + 1)
                dve.wait_ge(begun, 1)
                dve.wait_ge(st1_ready, count)
                dve.bn_aggr(mv1[0:a.n, :], st1[0:a.n, :]).then_inc(mv1_ready, 1)

            def embed_norm(a):
                dve.wait_ge(mv1_ready, a.no + 1)
                dve.scalar_tensor_tensor(lnc[0:a.n, :], lin[0:a.n, :], mv1[0:a.n, 0:1], lnw[0:a.n, :],
                                         ALU.subtract, ALU.mult).then_inc(lnc_ready, 1)
                dve.wait_ge(lnc_ready, a.no + 1)
                dve.wait_ge(rs1_ready, a.no + 1)
                if due(a.no - 1):
                    dve.wait_ge(hb_ready, a.no - 1)
                dve.scalar_tensor_tensor(h[0:a.n, a.par, :], lnc[0:a.n, :], rs1[0:a.n, :], lnb[0:a.n, :],
                                         ALU.mult, ALU.add).then_inc(h_ready, 1)
                dve.wait_ge(h_ready, a.no + 1)
                dve.bn_stats(st2[0:a.n, :], h[0:a.n, a.par, :]).then_inc(st2_ready, 1)
                count = held(dve, a.no + 1)
                dve.wait_ge(begun, 1)
                dve.wait_ge(st2_ready, count)
                dve.bn_aggr(mv2[0:a.n, :], st2[0:a.n, :]).then_inc(mv2_ready, 1)

            def centre(a):
                dve.wait_ge(mv2_ready, a.no + 1)
                dve.wait_ge(rs2_ready, a.no + 1)
                dve.scalar_tensor_tensor(xc[0:a.n, :], h[0:a.n, a.par, :], mv2[0:a.n, 0:1], gam[0:a.n, :],
                                         ALU.subtract, ALU.mult).then_inc(xc_ready, 1)
                dve.wait_ge(xc_ready, a.no + 1)
                dve.scalar_tensor_tensor(xf[0:a.n, :], xc[0:a.n, :], rs2[0:a.n, :], bet[0:a.n, :],
                                         ALU.mult, ALU.add).then_inc(xf_ready, 1)
                dve.wait_ge(xf_ready, a.no + 1)
                if due(a.no):
                    dve.wait_ge(xc_turned, a.no)
                dve.tensor_copy(xs[0:a.n, HIGH], xf[0:a.n, :]).then_inc(xs_high, 1)
                dve.wait_ge(xs_high, a.no + 1)
                for low, cols in LOWS:
                    op = dve.tensor_tensor(xs[0:a.n, low], xf[0:a.n, cols], xs[0:a.n, cols], ALU.subtract)
                op.then_inc(xs_ready, 1)

            def scores_less_max(g, u):
                no, buf = unit_of(g, u)
                dve.wait_ge(score_done, no + 1)
                dve.tensor_reduce(nmax[0:g.n, buf, :].rearrange("p (e j) -> p e j", e=2), scores_view(g.n), AX.X,
                                  ALU.max, negate=True).then_inc(max_ready, 1)
                dve.wait_ge(max_ready, no + 1)
                if due(no - 1):
                    dve.wait_ge(prob_turned, no - 1)
                dve.tensor_tensor(prob_view(prob, buf, g.n), scores_view(g.n),
                                  nmax[0:g.n, buf, :].rearrange("p (e j) -> p e j", e=2).unsqueeze(3)
                                  .to_broadcast([g.n, 2, 2, g.n]), ALU.add).then_inc(diff_ready, 1)

            def context(g, u):
                no, buf = unit_of(g, u)
                both = ctx_ps[0:g.n, 0:UH * (DH + 1)].rearrange("p (c t) -> p c t", c=UH)
                dve.wait_ge(av_done, no + 1)
                dve.reciprocal(rsum[0:g.n, :].unsqueeze(2), both[:, :, DH:DH + 1]).then_inc(rsum_ready, 1)
                dve.wait_ge(rsum_ready, no + 1)
                if due(no - 1):
                    dve.wait_ge(ctx_turned, no - 1)
                dve.tensor_tensor(cx[0:g.n, buf, :, :], both[:, :, 0:DH],
                                  rsum[0:g.n, :].unsqueeze(2).to_broadcast([g.n, UH, DH]),
                                  ALU.mult).then_inc(ctx_ready, 1)

            def residual(d):
                dve.wait_ge(proj_done, d.no + 1)
                dve.wait_ge(hb_ready, d.no + 1)
                if due(d.no - 1):
                    dve.wait_ge(base_ready, d.no - 1)
                dve.tensor_tensor(h2[0:d.n, d.par, :], tok_ps[0:d.n, 0:D],
                                  hb_all[0:d.n, bass.ds(d.no, 1), :].rearrange("p a n -> p (a n)"),
                                  ALU.add).then_inc(h2_ready, 1)
                dve.wait_ge(h2_ready, d.no + 1)
                dve.bn_stats(st4[0:d.n, :], h2[0:d.n, d.par, :]).then_inc(st4_ready, 1)
                count = held(dve, d.no + 1)
                dve.wait_ge(begun, 1)
                dve.wait_ge(st4_ready, count)
                dve.bn_aggr(mv4[0:d.n, :], st4[0:d.n, :]).then_inc(mv4_ready, 1)

            def norm_z(d):
                dve.wait_ge(mv4_ready, d.no + 1)
                dve.wait_ge(rs4_ready, d.no + 1)
                if due(d.no - 1):
                    dve.wait_ge(z_turned, d.no - 1)
                dve.tensor_scalar(z[0:d.n, d.par, :], h2[0:d.n, d.par, :], mv4[0:d.n, 0:1], rs4[0:d.n, :],
                                  ALU.subtract, ALU.mult).then_inc(z_ready, 1)

            def choose(d):
                n, logits = d.n, tok_ps[0:d.n, 256:256 + EXPERTS]
                count = held(dve, d.no + 1)
                dve.wait_ge(begun, 1)
                dve.wait_ge(logits_done, count)
                dve.max(top[0:n, :], logits).then_inc(top_ready, 1)
                count = held(dve, d.no + 1)
                dve.wait_ge(begun, 1)
                dve.wait_ge(top_ready, count)
                dve.max_index(top_i[0:n, :], top[0:n, :], logits).then_inc(top_i_ready, 1)
                dve.tensor_scalar(ldiff[0:n, 0:EXPERTS], logits, top[0:n, 0:1], None, ALU.subtract)
                dve.tensor_scalar(ldiff[0:n, EXPERTS:], top[0:n, 0:TOPK], top[0:n, 0:1], None,
                                  ALU.subtract).then_inc(ldiff_ready, 1)
                dve.wait_ge(top_i_ready, d.no + 1)
                dve.tensor_copy(top_e[0:n, :], top_i[0:n, 0:TOPK]).then_inc(top_e_ready, 1)
                dve.wait_ge(top_e_ready, d.no + 1)
                for k in range(TOPK):
                    op = dve.tensor_scalar(onehot[0:n, k, :], experts[0:n, :], top_e[0:n, k:k + 1], None, ALU.is_equal)
                op.then_inc(onehot_ready, 1)
                dve.wait_ge(onehot_ready, d.no + 1)
                if due(d.no - 1):
                    dve.wait_ge(rank_done, d.no - 1)
                dve.tensor_tensor(chosen[0:n, d.par, :], onehot[0:n, 0, :], onehot[0:n, 1, :],
                                  ALU.add).then_inc(chosen_ready, 1)
                dve.wait_ge(chosen_ready, d.no + 1)
                if due(d.no):
                    dve.wait_ge(seen_ready, d.no)
                if due(d.no):
                    dve.wait_ge(rank_done, d.no)
                dve.tensor_tensor(seen[0:n, 1 - d.par, :], seen[0:n, d.par, :], chosen[0:n, d.par, :],
                                  ALU.add).then_inc(seen_ready, 1)

            def gates(d):
                dve.wait_ge(lexp_ready, d.no + 1)
                dve.tensor_reduce(lsum[0:d.n, :], lexp[0:d.n, 0:EXPERTS], AX.X, ALU.add).then_inc(lsum_ready, 1)
                dve.wait_ge(lsum_ready, d.no + 1)
                dve.reciprocal(lrec[0:d.n, :], lsum[0:d.n, :]).then_inc(lrec_ready, 1)
                dve.wait_ge(lrec_ready, d.no + 1)
                dve.tensor_scalar(gates_all[0:d.n, bass.ds(d.no, 1), :].rearrange("p a n -> p (a n)"),
                                  lexp[0:d.n, EXPERTS:], lrec[0:d.n, :], None, ALU.mult).then_inc(gates_ready, 1)

            def low(buf, n):
                dve.wait_ge(w1_high, n * 2 + 2)
                dve.tensor_tensor(w1_s[:, buf, 1, :, :].rearrange("p c n -> p (c n)"), w1_stage[:, buf, :],
                                  w1_s[:, buf, 0, :, :].rearrange("p c n -> p (c n)"), ALU.subtract).then_inc(w1_low, 1)

            def slots(d):
                n = d.n
                dve.wait_ge(rank_done, d.no + 1)
                if due(d.no):
                    dve.wait_ge(rank_ready, d.no)
                dve.tensor_tensor(rank_e[0:n, :, :], onehot[0:n, :, :],
                                  tok_ps[0:n, 288:288 + EXPERTS].unsqueeze(1).to_broadcast([n, TOPK, EXPERTS]),
                                  ALU.mult).then_inc(rank_ready, 1)
                dve.wait_ge(rank_ready, d.no + 1)
                dve.tensor_reduce(rank[0:n, :], rank_e[0:n, :, :], AX.X, ALU.add).then_inc(rank_i_ready, 1)
                dve.wait_ge(rank_i_ready, d.no * 2 + 1)
                dve.tensor_copy(rank_i[0:n, :], rank[0:n, :]).then_inc(rank_i_ready, 1)
                dve.wait_ge(rank_i_ready, d.no * 2 + 2)
                dve.tensor_scalar(block_i[0:n, :], rank_i[0:n, :], 7, None,
                                  ALU.logical_shift_right).then_inc(block_ready, 1)
                dve.tensor_scalar(rank_w[0:n, :], rank[0:n, :], float(ROW), None, ALU.mult).then_inc(slot_f_ready, 1)
                dve.wait_ge(slot_f_ready, d.no * 2 + 1)
                dve.scalar_tensor_tensor(slot_f[0:n, :], top_e[0:n, :], float(QS), rank_w[0:n, :], ALU.mult,
                                         ALU.add).then_inc(slot_f_ready, 1)
                dve.wait_ge(block_ready, d.no + 1)
                dve.wait_ge(slot_f_ready, d.no * 2 + 2)
                if due(d.half * (16 * TOPK)):
                    dve.wait_ge(scattered[d.par], d.half * (16 * TOPK))
                dve.scalar_tensor_tensor(slot[0:n, d.par, :], block_i[0:n, :], float(1 - P * ROW), slot_f[0:n, :],
                                         ALU.mult, ALU.add).then_inc(slot_ready, 1)

            def iteration(at, i):
                g, d, b, a = (Group(at + k, i) for k in (0, -1, 1, 2))
                if g.live:
                    scores_less_max(g, 1)
                if d.live:
                    residual(d)
                if g.live:
                    context(g, 0)
                if d.live:
                    norm_z(d)
                if a.live:
                    embed_stats(a)
                if g.live:
                    scores_less_max(g, 2)
                if a.live:
                    embed_norm(a)
                if g.live:
                    context(g, 1)
                if a.live:
                    centre(a)
                if at == -2:
                    for piece, (c, cols) in enumerate(QKV_PIECES[:2]):
                        dve.wait_ge(qkv_high, piece + 1)
                        dve.tensor_tensor(wqkv[:, 1, c, cols], stage[:, c, cols], wqkv[:, 0, c, cols],
                                          ALU.subtract).then_inc(qkv_low, 1)
                if d.live:
                    choose(d)
                if b.live:
                    scores_less_max(b, 0)
                if g.live:
                    context(g, 2)
                if d.live:
                    slots(d)
                    gates(d)
                if at == GROUPS - 1:
                    low(0, 0)

            for e in range(1, EXPERTS):
                if e == 1:
                    dve.wait_ge(const, CONSTS + 5)
                op = dve.memset(experts[:, e:e + 1], float(e))
            op.then_inc(const, 1)
            dve.wait_ge(const, CONSTS + 6)
            dve.wait_ge(rows_in, 16 * 6)
            pipeline(dve, iteration)

            dve.wait_ge(count_done, 1)
            dve.tensor_reduce(most[:, :], turn_ps[0:1, 256:256 + EXPERTS], AX.X, ALU.max).then_inc(most_ready, 1)
            dve.wait_ge(most_ready, 1)
            dve.tensor_scalar(most_i[:, :], most[:, :], float(WINDOW - 1), None, ALU.add).then_inc(most_i_ready, 1)
            dve.wait_ge(most_i_ready, 1)
            dve.tensor_scalar(rounds[:, :], most_i[:, :], 8, None, ALU.logical_shift_right).then_inc(rounds_ready, 1)
            dve.wait_ge(table_in, 16)
            dve.tensor_scalar(table_h[:, :], table[:, :], 1, None, ALU.logical_shift_right).then_inc(halved, 1)
            dve.wait_ge(halved, 1)
            dve.tensor_scalar(table_z[:, :], table_h[:, :], float(TOKENS - 1), None, ALU.min).then_inc(rows_ready, 1)

            def turned(buf, steps, before_last=0):
                dve.wait_ge(zg_turned, steps + 1)
                if not isinstance(steps, int):
                    dve.wait_ge(hid_done, before_last * 3 + HID0)
                dve.tensor_copy(xt[:, buf, :, :],
                                turn16_ps[:, 0:3 * WINDOW].rearrange("p (c t) -> p c t", c=3)).then_inc(xt_ready, 1)

            dve.wait_ge(b2_in, 16)
            turned(0, 0)
            dve.sem_inc(y_ready, Y0)
            dve.wait_ge(rounds_ready, 1)
            with dve.Fori(0, dve.value_load(rounds[0:1, 0:1], min_val=1, max_val=ROUNDS)) as r:
                with dve.Fori(0, EXPERTS // 2) as j:
                    for buf in range(2):
                        n = r * EXPERTS + j * 2 + buf
                        low(1 - buf, n + 1)
                        turned(1 - buf, n + 1, n)
                        dve.wait_ge(y_done, n + 1 + Y0)
                        dve.wait_ge(to_ready, n + TO0)
                        dve.tensor_tensor(y[:, buf, :, :],
                                          score_ps[:, buf, 0:WT * D].rearrange("p (t n) -> p t n", t=WT),
                                          b2all[:, bass.ds(j * 2 + buf, 1), :].to_broadcast([P, WT, D]),
                                          ALU.add).then_inc(y_ready, 1)

            dve.wait_ge(base_ready, GROUPS)
            for k, (first, last) in enumerate(CHUNKS):
                dve.wait_ge(y_in[k], 16)
                for at in range(first, last):
                    n = Group(at).n
                    dve.scalar_tensor_tensor(part[0:n, at, :], y_back[0:n, at, 0:D], gates_all[0:n, at, 0:1],
                                             base_all[0:n, at, :], ALU.mult, ALU.add).then_inc(part_ready, 1)
                n = Group(first).n
                dve.wait_ge(part_ready, last)
                dve.wait_ge(second_ready, last)
                dve.tensor_tensor(part[0:n, first:last, :], part[0:n, first:last, :], second[0:n, first:last, :],
                                  ALU.add).then_inc(result_ready, 1)

        @block.tensor
        def _(pe):
            def embed(a):
                pe.wait_ge(patch_in[a.par], a.half * 16 + 16)
                if due(a.no - 2):
                    pe.wait_ge(h2_ready, a.no - 2)
                if due(a.no):
                    pe.wait_ge(lin_ready, a.no)
                for k in range(PK):
                    mm = pe.matmul(tok_ps[0:a.n, 0:D], patch[:, a.par, k * a.n:(k + 1) * a.n], tokw[:, k, :],
                                   start=k == 0, stop=k == PK - 1)
                mm.then_inc(embed_done, 1)

            def split_products(o, weights, tokens, flip=False):
                steps = [(weights(0, 0), tokens(0)), (weights(0, 0), tokens(1)), (weights(1, 0), tokens(0)),
                         (weights(0, 1), tokens(2)), (weights(1, 1), tokens(2))]
                for k, (w, x) in enumerate(steps):
                    left, right = (x, w) if flip else (w, x)
                    mm = pe.matmul(o, left, right, start=k == 0, stop=k == len(steps) - 1)
                return mm

            def turn16(n, src, t, width):
                for k, cols in enumerate((slice(0, P), slice(2 * P, 3 * P), slice(P, 2 * P))):
                    mm = pe.transpose(turn16_ps[:, k * width + t:k * width + t + n], src[:, cols], ident16[0:n, 0:n])
                return mm

            def turn(n, src):
                pe.transpose(turn_ps[:, 0:n], src[:, 0:P], ident[0:n, 0:n])
                return pe.transpose(turn_ps[0:DB, P:P + n], src[:, P:D], ident[0:n, 0:n])

            def turn_xc(a):
                pe.wait_ge(xs_ready, a.no + 1)
                if due(a.no):
                    pe.wait_ge(xn_ready, a.no)
                if due(a.no - 2):
                    pe.wait_ge(zt_ready, a.no - 2)
                turn16(a.n, xs[0:a.n, :], 0, GROUP).then_inc(xc_turned, 1)

            def fill(b, f):
                ps = fill_ps[(b.par + f) % 2]
                pe.wait_ge(xn_ready, b.no + 1)
                if due(b.no * FILLS + (f - 1)):
                    pe.wait_ge(fill_read, b.no * FILLS + (f - 1))
                tokens = lambda c: xn[:, b.par, c, 0:b.n]
                if f < UNITS:
                    for c in range(UH):
                        at = (c // 2) * INNER + (2 * f + c % 2) * P
                        mm = split_products(ps[:, c * GROUP:c * GROUP + b.n], lambda low, c: wqkv[:, low, c, at:at + P],
                                            tokens)
                else:
                    width = INNER // 2
                    at = 2 * INNER + (f - UNITS) * width
                    mm = split_products(ps[0:b.n, 0:width], lambda low, c: wqkv[:, low, c, at:at + width], tokens,
                                        flip=True)
                mm.then_inc(fill_done, 1)

            def scores(g, u):
                no, _ = unit_of(g, u)
                pe.wait_ge(fill_read, g.no * FILLS + (u + 1))
                if due(no):
                    pe.wait_ge(diff_ready, no)
                for e in range(2):
                    pe.matmul(score_ps[0:g.n, e, 0:2 * GROUP], mask_l[:, 0:g.n],
                              mask_r[:, :, :].rearrange("p j s -> p (j s)"), start=True, stop=False,
                              skip_group_check=True)
                for e in range(2):
                    for j in range(2):
                        rows = slice(DH * e, DH * e + DH)
                        mm = pe.matmul(score_ps[0:g.n, e, j * GROUP:j * GROUP + g.n], qk[rows, g.par, u, j, 0:g.n],
                                       qk[rows, g.par, u, 2 + j, 0:g.n], start=False, stop=True, skip_group_check=True)
                mm.then_inc(score_done, 1)

            def turn_prob(g, u):
                no, buf = unit_of(g, u)
                pe.wait_ge(exp_ready, no + 1)
                if due(no):
                    pe.wait_ge(prob_t_ready, no)
                for c in range(UH):
                    mm = pe.transpose(prob_ps[0:g.n, c * GROUP:c * GROUP + g.n], prob[0:g.n, buf, c, 0:g.n],
                                      ident[0:g.n, 0:g.n])
                mm.then_inc(prob_turned, 1)

            def attend(g, u):
                no, buf = unit_of(g, u)
                pe.wait_ge(prob_t_ready, no + 1)
                pe.wait_ge(fill_read, g.no * FILLS + FILLS)
                if due(no):
                    pe.wait_ge(ctx_t_ready, no)
                for c in range(UH):
                    e, j = divmod(c, 2)
                    at = 2 * j + e
                    mm = pe.matmul(ctx_ps[0:g.n, at * (DH + 1):(at + 1) * (DH + 1)], prob_t[0:g.n, buf, c, 0:g.n],
                                   v[0:g.n, g.par, UH * u + at, :], start=True, stop=True)
                mm.then_inc(av_done, 1)

            def turn_ctx(g, u):
                no, buf = unit_of(g, u)
                pe.wait_ge(ctx_ready, no + 1)
                for j in range(2):
                    at = UH * (DH + 1) + j * GROUP
                    mm = pe.transpose(ctx_ps[:, at:at + g.n],
                                      cx[0:g.n, buf, 2 * j:2 * j + 2, :].rearrange("p c t -> p (c t)"),
                                      ident[0:g.n, 0:g.n])
                mm.then_inc(ctx_turned, 1)

            def project(g):
                pe.wait_ge(ctx_t_ready, g.no * UNITS + UNITS)
                pe.wait_ge(lin_ready, min(g.no + 3, GROUPS) if isinstance(g.no, int) else g.no + 3)
                if due(g.no):
                    pe.wait_ge(rank_ready, g.no)
                for k in range(PK):
                    mm = pe.matmul(tok_ps[0:g.n, 0:D], cx_t[:, g.par, k, 0:g.n], wo[:, k, :],
                                   start=k == 0, stop=k == PK - 1)
                mm.then_inc(proj_done, 1)

            def turn_z(d):
                pe.wait_ge(z_ready, d.no + 1)
                pe.wait_ge(xn_ready, min(d.no + 3, GROUPS) if isinstance(d.no, int) else d.no + 3)
                turn(d.n, z[0:d.n, d.par, :]).then_inc(z_turned, 1)

            def logits(d):
                pe.wait_ge(zt_ready, d.no + 1)
                pe.wait_ge(lin_ready, min(d.no + 4, GROUPS) if isinstance(d.no, int) else d.no + 4)
                pe.matmul(tok_ps[0:d.n, 256:256 + EXPERTS], zt_a[:, 0:d.n], wr_a[:, :], start=True, stop=False)
                pe.matmul(tok_ps[0:d.n, 256:256 + EXPERTS], zt_b[0:KB, 0:d.n], wr_b[0:KB, :], start=False,
                          stop=True).then_inc(logits_done, 1)

            def ranks(d):
                pe.wait_ge(chosen_ready, d.no + 1)
                if due(d.no):
                    pe.wait_ge(seen_ready, d.no)
                pe.wait_ge(ldiff_ready, d.no + 1)
                pe.wait_ge(top_i_ready, d.no + 1)
                o = tok_ps[0:d.n, 288:288 + EXPERTS]
                pe.matmul(o, before[0:d.n, 0:d.n], chosen[0:d.n, d.par, :], start=True, stop=False)
                pe.matmul(o, ones[:, 0:d.n], seen[:, d.par, :], start=False, stop=True).then_inc(rank_done, 1)

            def iteration(at, i):
                g, d, b, a = (Group(at + k, i) for k in (0, -1, 1, 2))
                if at == -1:
                    pe.wait_ge(qkv_low, 2)
                if at == 0:
                    pe.wait_ge(wo_in, 48)
                if d.live:
                    turn_ctx(d, 2)
                if g.live:
                    scores(g, 1)
                    turn_prob(g, 0)
                if d.live:
                    project(d)
                if g.live:
                    attend(g, 0)
                if a.live and at != -1:
                    embed(a)
                if at == -2:
                    embed(Group(1))
                if g.live:
                    scores(g, 2)
                    turn_ctx(g, 0)
                    turn_prob(g, 1)
                if b.live:
                    fill(b, 0)
                if d.live:
                    turn_z(d)
                if g.live:
                    attend(g, 1)
                if b.live:
                    fill(b, 1)
                if d.live:
                    logits(d)
                if b.live:
                    scores(b, 0)
                if g.live:
                    turn_ctx(g, 1)
                    turn_prob(g, 2)
                if b.live:
                    fill(b, 2)
                if g.live:
                    attend(g, 2)
                if d.live:
                    ranks(d)
                if b.live:
                    if at == -1:
                        pe.wait_ge(v_low, 2)
                    fill(b, 3)
                if a.live:
                    turn_xc(a)
                if b.live:
                    fill(b, 4)

            pe.wait_ge(tokw_in, 16)
            pe.wait_ge(const, CONSTS + 6)
            pipeline(pe, iteration)

            final = Group(GROUPS - 1)
            pe.wait_ge(seen_ready, GROUPS)
            pe.matmul(turn_ps[0:1, 256:256 + EXPERTS], ones[:, 0:1], seen[:, 1 - final.par, :],
                      start=True, stop=True).then_inc(count_done, 1)

            def turn_tokens(buf, half, n):
                pe.wait_ge(zg_in[buf], half * (16 * WT) + 16 * WT)
                if due(n):
                    pe.wait_ge(xt_ready, n)
                for t in range(WT):
                    mm = turn16(P, zg[:, buf, t, :], t * P, WINDOW)
                mm.then_inc(zg_turned, 1)

            pe.sem_inc(hid_done, HID0)
            turn_tokens(0, 0, 0)
            pe.sem_inc(y_done, Y0)
            pe.wait_ge(rounds_ready, 1)
            with pe.Fori(0, pe.value_load(rounds[0:1, 0:1], min_val=1, max_val=ROUNDS)) as r:
                with pe.Fori(0, EXPERTS // 2) as j:
                    for buf in range(2):
                        n = r * EXPERTS + j * 2 + buf
                        half = r * (EXPERTS // 2) + j
                        pe.wait_ge(xt_ready, n + 1)
                        pe.wait_ge(w1_low, n + 1)
                        for c in range(FK // 2):
                            pe.wait_ge(gelu_ready, n * 3 + (c - 2 + GELU0))
                            for k in (2 * c, 2 * c + 1):
                                o = hid_ps[c][:, (k % 2) * WINDOW:(k % 2 + 1) * WINDOW]
                                cols = slice(k * P, (k + 1) * P)
                                mm = split_products(o, lambda low, c: w1_s[:, buf, low, c, cols],
                                                    lambda c: xt[:, buf, c, :])
                            mm.then_inc(hid_done, 1)
                        turn_tokens(1 - buf, half + buf, n + 1)
                        pe.wait_ge(y_ready, n - 1 + Y0)
                        pe.wait_ge(w2_in[buf], half * 16 + 16)
                        for t in range(WT):
                            for k in range(FK):
                                if t == 0 and k % 2 == 0:
                                    pe.wait_ge(gelu_ready, n * 3 + (k // 2 + 1 + GELU0))
                                mm = pe.matmul(score_ps[:, buf, t * D:(t + 1) * D], hid[:, buf, k, t * P:(t + 1) * P],
                                               w2_s[:, buf, k * D:(k + 1) * D], start=k == 0, stop=k == FK - 1)
                        mm.then_inc(y_done, 1)


INPUTS = ["patches", "patches_last", "tok_w", "tok_b", "tok_ln_w", "tok_ln_b", "gamma", "beta", "w_qkv", "w_out",
          "b_out", "w_router", "w1", "w2", "b2"]


def kernel(x, L0_tok_W, L0_tok_b, L0_tok_ln_w, L0_tok_ln_b, L0_attn_ln_gamma, L0_attn_ln_beta, L0_attn_w_qkv,
           L0_attn_w_out, L0_attn_b_out, L0_ffn_wr, L0_ffn_w1, L0_ffn_b1, L0_ffn_w2, L0_ffn_b2):
    import numpy as np
    import concourse.bacc as bacc
    from concourse.bass_utils import run_bass_kernel_spmd

    def chunked(w):
        w = np.asarray(w)
        return w.T.reshape(-1, P, w.shape[0]).transpose(1, 0, 2).reshape(P, -1)

    def rows_twice(w):
        return np.concatenate([w[..., 0:P, :], np.concatenate([w[..., P:D, :]] * 2, axis=-2)], axis=-1)

    G1 = GROUPS - 1
    feats = np.asarray(x).reshape(IMAGES, 3, 6, 16, 6, 16).transpose(1, 3, 5, 0, 2, 4).reshape(PK, P, TOKENS)
    arrays = {
        "patches": feats[:, :, :G1 * GROUP].reshape(PK, P, G1, GROUP).transpose(2, 1, 0, 3).reshape(G1, P, -1),
        "patches_last": feats[:, :, G1 * GROUP:].transpose(1, 0, 2).reshape(P, -1),
        "tok_w": chunked(L0_tok_W),
        "tok_b": L0_tok_b, "tok_ln_w": L0_tok_ln_w, "tok_ln_b": L0_tok_ln_b,
        "gamma": L0_attn_ln_gamma, "beta": L0_attn_ln_beta,
        "w_qkv": rows_twice(np.asarray(L0_attn_w_qkv).T),
        "w_out": chunked(L0_attn_w_out), "b_out": L0_attn_b_out,
        "w_router": np.asarray(L0_ffn_wr).T,
        "w1": rows_twice(np.asarray(L0_ffn_w1).transpose(0, 2, 1)),
        "w2": np.concatenate([
            np.asarray(L0_ffn_w2).reshape(EXPERTS, D, FK, P).transpose(0, 3, 2, 1).reshape(EXPERTS, P, -1),
            np.asarray(L0_ffn_b1).reshape(EXPERTS, FK, P).transpose(0, 2, 1)], axis=2),
        "b2": L0_ffn_b2,
    }
    nc = bacc.Bacc("TRN2", target_bir_lowering=False, num_devices=1)
    given, args = {}, []
    for name in INPUTS:
        a = np.ascontiguousarray(arrays[name])
        given[f"in_{name}"] = a
        args.append(nc.dram_tensor(f"in_{name}", a.shape, mybir.dt.from_np(a.dtype), kind="ExternalInput").ap())
    args.append(nc.dram_tensor("out_0", (TOKENS, D), F32, kind="ExternalOutput").ap())
    vit_block(nc, *args)
    r = run_bass_kernel_spmd(nc, [given], core_ids=[0])
    return r.results[0]["out_0"].reshape(IMAGES, IMAGE, D)
```
